# Optimizing a Trainium2 kernel written in Bass

```python
import numpy as np
import jax
import jax.numpy as jnp

def _softmax(x, axis=-1):
    return jax.nn.softmax(x, axis=axis)

def _gelu(x):
    return jax.nn.gelu(x, approximate=True)

def _silu(x):
    return jax.nn.silu(x)

def _sigmoid(x):
    return jax.nn.sigmoid(x)

def _layernorm(x, axis=-1, eps=1e-05):
    m = jnp.mean(x, axis=axis, keepdims=True)
    v = jnp.var(x, axis=axis, keepdims=True)
    return (x - m) / jnp.sqrt(v + eps)

def _scatter_add(tgt, idx, src, axis=0):
    return tgt.at[idx].add(src)

def _segment_sum(src, seg, n):
    return jax.ops.segment_sum(src, seg, n)
kernel_name = 'mk_macaron_d1_jaxref_r8_5804a2'

def setup_inputs(seed: int=0):
    np.random.seed(seed)
    _w = jnp.asarray

    def _L0_attn_setup():
        import jax, jax.numpy as jnp
        import numpy as np
        D = 128
        H = 16
        HKV = 4
        HD = D // H
        L = 64
        EPS = 1e-06
        LN_EPS = 1e-05
        B, S = (2, 128)

        def _feat(x):
            return jax.nn.elu(x) + 1.0
        key = jax.random.key(seed)
        ks = jax.random.split(key, 8)
        w = lambda k, shape: jax.random.normal(k, shape, jnp.float32) * 0.02
        return {'x': jax.random.normal(ks[0], (B, S, D), jnp.float32), 'Wq': w(ks[1], (D, D)), 'bq': jnp.zeros((D,), jnp.float32), 'Wk': w(ks[2], (D, HKV * HD)), 'bk': jnp.zeros((HKV * HD,), jnp.float32), 'Wv': w(ks[3], (D, HKV * HD)), 'bv': jnp.zeros((HKV * HD,), jnp.float32), 'Wc': w(ks[4], (HKV * HD, L)), 'We': w(ks[5], (L, HKV * HD)), 'Wo': w(ks[6], (D, D)), 'bo': jnp.zeros((D,), jnp.float32), 'gamma': jnp.ones((D,), jnp.float32), 'beta': jnp.zeros((D,), jnp.float32)}
    _L0_attn_in = _L0_attn_setup()

    def _L0_ffn_setup():
        import jax, jax.numpy as jnp
        import numpy as np
        TOP_K = 2
        ROUTE_SCALE = 1.0
        EPS = 1e-20
        B, S, D = (2, 64, 128)
        E = 8
        F = 96
        FS = 96 * 1
        key = jax.random.key(seed)
        ks = jax.random.split(key, 9)
        s = 0.02
        return {'hidden_states': jax.random.normal(ks[0], (B, S, D), dtype=jnp.float32), 'W_gate_router': jax.random.normal(ks[1], (D, E), dtype=jnp.float32) * s, 'expert_bias': jnp.zeros((E,), dtype=jnp.float32), 'Wg': jax.random.normal(ks[2], (E, D, F), dtype=jnp.float32) * s, 'Wu': jax.random.normal(ks[3], (E, D, F), dtype=jnp.float32) * s, 'Wd': jax.random.normal(ks[4], (E, F, D), dtype=jnp.float32) * s, 'Wg_s': jax.random.normal(ks[5], (D, FS), dtype=jnp.float32) * s, 'Wu_s': jax.random.normal(ks[6], (D, FS), dtype=jnp.float32) * s, 'Wd_s': jax.random.normal(ks[7], (FS, D), dtype=jnp.float32) * s}
    _L0_ffn_in = _L0_ffn_setup()
    _d = {'L0_attn_x': _L0_attn_in['x'], 'L0_attn_Wq': _L0_attn_in['Wq'], 'L0_attn_bq': _L0_attn_in['bq'], 'L0_attn_Wk': _L0_attn_in['Wk'], 'L0_attn_bk': _L0_attn_in['bk'], 'L0_attn_Wv': _L0_attn_in['Wv'], 'L0_attn_bv': _L0_attn_in['bv'], 'L0_attn_Wc': _L0_attn_in['Wc'], 'L0_attn_We': _L0_attn_in['We'], 'L0_attn_Wo': _L0_attn_in['Wo'], 'L0_attn_bo': _L0_attn_in['bo'], 'L0_attn_gamma': _L0_attn_in['gamma'], 'L0_attn_beta': _L0_attn_in['beta'], 'L0_ffn_W_gate_router': _L0_ffn_in['W_gate_router'], 'L0_ffn_expert_bias': _L0_ffn_in['expert_bias'], 'L0_ffn_Wg': _L0_ffn_in['Wg'], 'L0_ffn_Wu': _L0_ffn_in['Wu'], 'L0_ffn_Wd': _L0_ffn_in['Wd'], 'L0_ffn_Wg_s': _L0_ffn_in['Wg_s'], 'L0_ffn_Wu_s': _L0_ffn_in['Wu_s'], 'L0_ffn_Wd_s': _L0_ffn_in['Wd_s']}
    _x0 = _d['L0_attn_x']
    _d['L0_attn_x'] = jax.random.normal(jax.random.fold_in(jax.random.key(seed), 1), (16, 256, 128), dtype=_x0.dtype)
    del _x0
    return _d

def reference(L0_attn_x, L0_attn_Wq, L0_attn_bq, L0_attn_Wk, L0_attn_bk, L0_attn_Wv, L0_attn_bv, L0_attn_Wc, L0_attn_We, L0_attn_Wo, L0_attn_bo, L0_attn_gamma, L0_attn_beta, L0_ffn_W_gate_router, L0_ffn_expert_bias, L0_ffn_Wg, L0_ffn_Wu, L0_ffn_Wd, L0_ffn_Wg_s, L0_ffn_Wu_s, L0_ffn_Wd_s):

    def _L0_attn_ref(x, Wq, bq, Wk, bk, Wv, bv, Wc, We, Wo, bo, gamma, beta):
        import jax, jax.numpy as jnp
        import numpy as np
        D = 128
        H = 16
        HKV = 4
        HD = D // H
        L = 64
        EPS = 1e-06
        LN_EPS = 1e-05
        B, S = (2, 128)

        def _feat(x):
            return jax.nn.elu(x) + 1.0
        b, s, _ = x.shape
        residual = x
        q = x @ Wq + bq
        k = x @ Wk + bk
        v = x @ Wv + bv
        k = k @ Wc @ We
        v = v @ Wc @ We
        q = q.reshape(b, s, H, HD).transpose(0, 2, 1, 3)
        k = k.reshape(b, s, HKV, HD).transpose(0, 2, 1, 3)
        v = v.reshape(b, s, HKV, HD).transpose(0, 2, 1, 3)
        rep = H // HKV
        k = jnp.repeat(k, rep, axis=1)
        v = jnp.repeat(v, rep, axis=1)
        qf = _feat(q)
        kf = _feat(k)
        kv = jnp.einsum('bhsf,bhsd->bhsfd', kf, v)
        kv_cum = jnp.cumsum(kv, axis=2)
        num = jnp.einsum('bhsf,bhsfd->bhsd', qf, kv_cum)
        den = jnp.einsum('bhsf,bhsf->bhs', qf, jnp.cumsum(kf, axis=2))[..., None] + EPS
        o = num / den
        o = o.transpose(0, 2, 1, 3).reshape(b, s, D)
        o = o @ Wo + bo
        y = residual + o
        mu = jnp.mean(y, axis=-1, keepdims=True)
        var = jnp.var(y, axis=-1, keepdims=True)
        return (y - mu) / jnp.sqrt(var + LN_EPS) * gamma + beta

    def _L0_ffn_ref(hidden_states, W_gate_router, expert_bias, Wg, Wu, Wd, Wg_s, Wu_s, Wd_s):
        import jax, jax.numpy as jnp
        import numpy as np
        TOP_K = 2
        ROUTE_SCALE = 1.0
        EPS = 1e-20
        B, S, D = (2, 64, 128)
        E = 8
        F = 96
        FS = 96 * 1
        b, s, d = hidden_states.shape
        x = hidden_states.reshape(-1, d)
        T = x.shape[0]
        logits = x @ W_gate_router
        scores = jax.nn.sigmoid(logits.astype(jnp.float32))
        _, sel = jax.lax.top_k(scores + expert_bias, TOP_K)
        top_scores = jnp.take_along_axis(scores, sel, axis=1)
        top_scores = top_scores / (top_scores.sum(-1, keepdims=True) + EPS)
        top_scores = top_scores * ROUTE_SCALE
        shared = jax.nn.silu(x @ Wg_s) * (x @ Wu_s) @ Wd_s
        tok = jnp.repeat(jnp.arange(T), TOP_K)
        exp = sel.reshape(-1)
        w = top_scores.reshape(-1)
        xr = x[tok]
        h = jax.nn.silu(jnp.einsum('nd,edf->enf', xr, Wg)) * jnp.einsum('nd,edf->enf', xr, Wu)
        out_all = jnp.einsum('enf,efd->end', h, Wd)
        routed = out_all[exp, jnp.arange(exp.shape[0])]
        routed = (routed.astype(jnp.float32) * w[:, None]).astype(hidden_states.dtype)
        out = shared.at[tok].add(routed)
        return out.reshape(b, s, d)
    x = L0_attn_x
    x = x + 0.5 * _L0_ffn_ref(_layernorm(x, axis=-1), L0_ffn_W_gate_router, L0_ffn_expert_bias, L0_ffn_Wg, L0_ffn_Wu, L0_ffn_Wd, L0_ffn_Wg_s, L0_ffn_Wu_s, L0_ffn_Wd_s)
    x = x + _L0_attn_ref(_layernorm(x, axis=-1), L0_attn_Wq, L0_attn_bq, L0_attn_Wk, L0_attn_bk, L0_attn_Wv, L0_attn_bv, L0_attn_Wc, L0_attn_We, L0_attn_Wo, L0_attn_bo, L0_attn_gamma, L0_attn_beta)
    x = x + 0.5 * _L0_ffn_ref(_layernorm(x, axis=-1), L0_ffn_W_gate_router, L0_ffn_expert_bias, L0_ffn_Wg, L0_ffn_Wu, L0_ffn_Wd, L0_ffn_Wg_s, L0_ffn_Wu_s, L0_ffn_Wd_s)
    return x

_drawn_inputs = setup_inputs


def setup_inputs(seed=0):
    import zlib

    import numpy as np

    out = dict(_drawn_inputs(seed))
    spreads = {'L0_attn_bq': (0.0, 2.0),
     'L0_attn_bk': (0.0, 2.0),
     'L0_attn_bv': (0.0, 0.8),
     'L0_attn_bo': (0.0, 0.406),
     'L0_attn_gamma': (1.0, 0.2),
     'L0_attn_beta': (0.0, 0.1),
     'L0_ffn_expert_bias': (0.0, 0.8)}
    factors = {'L0_attn_Wq': 8.0,
     'L0_attn_Wk': 8.0,
     'L0_attn_Wv': 8.0,
     'L0_attn_Wc': 8.0,
     'L0_attn_We': 8.0,
     'L0_attn_Wo': 8.0,
     'L0_ffn_W_gate_router': 8.0,
     'L0_ffn_Wg': 8.0,
     'L0_ffn_Wu': 8.0,
     'L0_ffn_Wd': 8.0,
     'L0_ffn_Wg_s': 8.0,
     'L0_ffn_Wu_s': 8.0,
     'L0_ffn_Wd_s': 8.0}
    for name, (base, spread) in spreads.items():
        noise = np.random.default_rng([zlib.crc32(name.encode()), seed]).standard_normal(out[name].shape)
        drawn = base * np.exp(spread * noise) if base else spread * noise
        out[name] = jnp.asarray(drawn.astype(out[name].dtype))
    for name, factor in factors.items():
        out[name] = (out[name] * factor).astype(out[name].dtype)
    return out
```

```python
from contextlib import ExitStack

import concourse.bass as bass
from concourse import mybir

ALU = mybir.AluOpType
ACT = mybir.ActivationFunctionType
F32 = mybir.dt.float32
F32R = mybir.dt.float32r
U32 = mybir.dt.uint32
AX_X = mybir.AxisListType.X

P = 128
LN_EPS = 1e-5
DEN_EPS = 1e-6
ROUTE_EPS = 1e-20
TILES = 4
CHUNK = TILES * P
STEPS = 7

Y_TABLE = [
    [("ffn_down_end", 0), ("ffn_out", 0)],
    [("ffn_outT", 0), ("ffn_add", 0), ("att_stat", 0), ("att_norm", 0), ("x_load", 0), ("x_copy", 0)],
    [("ffn_stat", 0), ("ffn_norm", 0), ("att_yT", 0), ("att_hi", 0), ("att_lo", 0)],
    [("att_qkv", 0), ("att_exp", 0), ("att_feat", 0), ("att_kv", 0), ("att_kv", 1), ("ffn_yT", 0), ("ffn_hi", 0),
     ("ffn_lo", 0)],
    [("att_qkv", 1), ("att_exp", 1), ("ffn_route", 0), ("ffn_exp", 0), ("att_feat", 1), ("ffn_sel", 0)],
    [("att_cum", 0), ("att_cum_copy", 0), ("att_mul", 0), ("ffn_wT", 0), ("ffn_wT_copy", 0), ("att_kv", 2),
     ("att_kv", 3)],
    [("att_cum", 1), ("att_cum_copy", 1), ("att_mul", 1), ("att_red", 0)],
]
X_TABLE = [
    [("ffn_down_end", 0), ("ffn_out", 0), ("att_cum", 2), ("att_cum_copy", 2), ("att_mul", 2), ("att_red", 1)],
    [("ffn_outT", 0), ("ffn_add", 0), ("att_cum", 3), ("att_cum_copy", 3), ("att_mul", 3), ("att_red", 2)],
    [("att_red", 3), ("att_div", 0)],
    [("att_oT", 0), ("att_o_hi", 0), ("att_o_lo", 0), ("att_proj", 0), ("att_res", 0), ("att_norm_z", 0)],
    [("att_x2", 0), ("ffn_stat", 0), ("ffn_norm", 0)],
    [("ffn_yT", 0), ("ffn_hi", 0), ("ffn_lo", 0)],
    [("ffn_route", 0), ("ffn_exp", 0), ("ffn_sel", 0), ("ffn_wT", 0), ("ffn_wT_copy", 0)],
]


def broadcast_free(ap, axis, n):
    names = [f"a{i}" for i in range(len(ap.shape))]
    new = names[:axis] + ["z"] + names[axis:]
    if axis < len(names):
        joined = names[:axis] + [f"(z {names[axis]})"] + names[axis + 1:]
    else:
        joined = names[:-1] + [f"({names[-1]} z)"]
    shape = list(ap.shape)
    shape.insert(axis, n)
    return ap.rearrange(f"{' '.join(joined)} -> {' '.join(new)}", z=1).to_broadcast(shape)


def macaron_kernel(nc, x, Wq, bq, Wk, bk, Wv, bv, Wc, We, Wo, bo, gamma, beta,
                   Wr, expert_bias, Wg, Wu, Wd, Wg_s, Wu_s, Wd_s, out):
    B, S, D = x.shape
    KV = Wk.shape[1]
    L = Wc.shape[1]
    E, _, FE = Wg.shape
    FS = Wg_s.shape[1]
    FR = E * FE
    HD = 8
    G = KV // HD
    H = D // HD
    R = H // G
    QKV = D + 2 * KV
    V1 = HD + 1
    KVC = G * HD * V1
    NCH = B * S // CHUNK
    assert D == P and FR % P == 0 and FR // P + 1 == STEPS and S == 2 * P and NCH >= 4

    x_dram = x.rearrange("b s d -> (b s) d").rearrange("(c i p) d -> c p i d", i=TILES, p=P)
    out_dram = out.rearrange("b s d -> (b s) d").rearrange("(c i p) d -> c p i d", i=TILES, p=P)

    with ExitStack() as ctx:
        def sb(name, shape, dt=F32):
            return ctx.enter_context(nc.sbuf_tensor(name, shape, dt))

        def sem(name):
            return ctx.enter_context(nc.semaphore(name))

        wg_raw, wu_raw = sb("wg_raw", [P, FR + FS]), sb("wu_raw", [P, FR + FS])
        wd = sb("wd", [P, STEPS, D])
        wr_raw = sb("wr_raw", [P, E])
        wqkv_raw = sb("wqkv_raw", [P, QKV])
        wkv_in = sb("wkv_in", [P, 2 * KV])
        wo_raw = sb("wo_raw", [P, D])
        wc_in, we_in = sb("wc_in", [KV, L]), sb("we_in", [L, KV])
        bkv_col = sb("bkv_col", [KV, 2])
        bias_raw = sb("bias_raw", [1, QKV + D])
        gamma_b, beta_b, ebias_b = sb("gamma_b", [P, D]), sb("beta_b", [P, D]), sb("ebias_b", [P, E])
        wg_hi, wg_lo = sb("wg_hi", [P, FR + FS], F32R), sb("wg_lo", [P, FR + FS], F32R)
        wu_hi, wu_lo = sb("wu_hi", [P, FR + FS], F32R), sb("wu_lo", [P, FR + FS], F32R)
        wr_hi, wr_lo = sb("wr_hi", [P, E], F32R), sb("wr_lo", [P, E], F32R)
        wqkv_hi, wqkv_lo = sb("wqkv_hi", [P, QKV], F32R), sb("wqkv_lo", [P, QKV], F32R)
        wo_hi, wo_lo = sb("wo_hi", [P, D], F32R), sb("wo_lo", [P, D], F32R)
        bias_hi, bias_lo = sb("bias_hi", [1, QKV + D], F32R), sb("bias_lo", [1, QKV + D], F32R)
        wcT, wkvT, wce = sb("wcT", [L, KV]), sb("wkvT", [KV, 2, P]), sb("wce", [KV, KV])
        ident, ones, tri = sb("ident", [P, P]), sb("ones", [P, P]), sb("tri", [P, P])
        ones_row = sb("ones_row", [1, P], F32R)
        spread_raw, spread = sb("spread_raw", [2 * E, FR]), sb("spread", [2 * E, FR], F32R)
        iota_e = sb("iota_e", [P, E])
        neg_half = sb("neg_half", [P, TILES])
        x_next, x_cur = sb("x_next", [P, TILES, D]), sb("x_cur", [P, TILES, D])
        x1, x1_beta, x2, y_out = (sb(n, [P, TILES, D]) for n in ("x1", "x1_beta", "x2", "y_out"))
        stats, moments, var_eps, neg_mean, rstd, normed = {}, {}, {}, {}, {}, {}
        for k in "FAZ":
            stats[k], moments[k] = sb(f"stats_{k}", [P, TILES, 6]), sb(f"moments_{k}", [P, TILES, 2])
            var_eps[k], neg_mean[k] = sb(f"var_eps_{k}", [P, TILES]), sb(f"neg_mean_{k}", [P, TILES])
            rstd[k], normed[k] = sb(f"rstd_{k}", [P, TILES]), sb(f"normed_{k}", [P, TILES, D])
        fyT_hi = [sb(f"fyT_hi{i}", [P, CHUNK], F32R) for i in range(2)]
        fyT_lo = [sb(f"fyT_lo{i}", [P, CHUNK], F32R) for i in range(2)]
        exp_neg, denom, score, biased = (sb(n, [P, TILES, E]) for n in ("exp_neg", "denom", "score", "biased"))
        top_val, top_idx = sb("top_val", [P, TILES, 8]), sb("top_idx", [P, TILES, 8], U32)
        is_first, is_second, chosen, picked = (
            sb(n, [P, TILES, E]) for n in ("is_first", "is_second", "chosen", "picked"))
        pick_sum, pick_inv = sb("pick_sum", [P, TILES]), sb("pick_inv", [P, TILES])
        pick_sum_eps = sb("pick_sum_eps", [P, TILES])
        route_w = sb("route_w", [P, TILES, E])
        route_parts = sb("route_parts", [P, TILES, 2 * E], F32R)
        wT = [sb(f"wT{i}", [2 * E, CHUNK], F32R) for i in range(2)]
        silu_g = [sb(f"silu_g{i}", [P, CHUNK]) for i in range(2)]
        gated = [sb(f"gated{i}", [P, CHUNK]) for i in range(2)]
        hidden = sb("hidden", [P, STEPS, CHUNK])
        downT = sb("downT", [P, CHUNK])
        ayT_hi, ayT_lo = sb("ayT_hi", [P, CHUNK], F32R), sb("ayT_lo", [P, CHUNK], F32R)
        qk_exp, qk_relu = sb("qk_exp", [P, TILES, D + KV]), sb("qk_relu", [P, TILES, D + KV])
        qk_feat = sb("qk_feat", [P, TILES, D + KV])
        v_ones = sb("v_ones", [P, TILES, G, V1])
        kv = sb("kv", [P, TILES, KVC])
        kv_cum = sb("kv_cum", [P, 2, KVC])
        prod = sb("prod", [P, 2, H * HD * V1])
        num_den = sb("num_den", [P, TILES, H, V1])
        den_eps, den_inv = sb("den_eps", [P, TILES, H]), sb("den_inv", [P, TILES, H])
        att_o = sb("att_o", [P, TILES, D])
        oT_hi, oT_lo = sb("oT_hi", [P, CHUNK], F32R), sb("oT_lo", [P, CHUNK], F32R)
        att_z, z_gamma = sb("att_z", [P, TILES, D]), sb("z_gamma", [P, TILES, D])
        def bank(name):
            return ctx.enter_context(nc.psum_tensor(name, [P, 512], F32))
        ps_gate, ps_up = [bank("ps_gate0"), bank("ps_gate1")], [bank("ps_up0"), bank("ps_up1")]
        ps_w, ps_down, ps_f, ps_a = bank("ps_w"), bank("ps_down"), bank("ps_f"), bank("ps_a")

        w_loaded, small_loaded = sem("w_loaded"), sem("small_loaded")
        x_loaded, x_copied = sem("x_loaded"), sem("x_copied")
        zeroed, masks_made, consts_made = sem("zeroed"), sem("masks_made"), sem("consts_made")
        dve_consts = sem("dve_consts")
        fold_ready, fold_copied = sem("fold_ready"), sem("fold_copied")
        hi_made, weights_split = sem("hi_made"), sem("weights_split")
        stats_made = {k: sem(f"stats_made_{k}") for k in "FAZ"}
        moments_made = {k: sem(f"moments_made_{k}") for k in "FAZ"}
        eps_added = {k: sem(f"eps_added_{k}") for k in "FAZ"}
        rstd_made = {k: sem(f"rstd_made_{k}") for k in "FAZ"}
        norm_made = {k: sem(f"norm_made_{k}") for k in "FAZ"}
        fyT_ready, fyT_hi_made, fyT_lo_made = sem("fyT_ready"), sem("fyT_hi_made"), sem("fyT_lo_made")
        logits_ready, exp_made, sel_chain, w_made = (
            sem("logits_ready"), sem("exp_made"), sem("sel_chain"), sem("w_made"))
        wT_ready, wT_copied = sem("wT_ready"), sem("wT_copied")
        gate_ready, up_ready, silu_made, gated_made, hidden_made = (
            sem("gate_ready"), sem("up_ready"), sem("silu_made"), sem("gated_made"), sem("hidden_made"))
        down_ready, down_copied, out_ready, out_added = (
            sem("down_ready"), sem("down_copied"), sem("out_ready"), sem("out_added"))
        ayT_ready, ayT_hi_made, ayT_lo_made = sem("ayT_ready"), sem("ayT_hi_made"), sem("ayT_lo_made")
        qkv_ready, qkv_read, feat_made = sem("qkv_ready"), sem("qkv_read"), sem("feat_made")
        kv_made, cum_ready, cum_copied, prod_made, red_made = (
            sem("kv_made"), sem("cum_ready"), sem("cum_copied"), sem("prod_made"), sem("red_made"))
        den_chain, o_made = sem("den_chain"), sem("o_made")
        oT_ready, oT_hi_made, oT_lo_made = sem("oT_ready"), sem("oT_hi_made"), sem("oT_lo_made")
        z_ready, z_added, z_scaled, x2_made, beta_added = (
            sem("z_ready"), sem("z_added"), sem("z_scaled"), sem("x2_made"), sem("beta_added"))
        out_stored = sem("out_stored")

        waits_passed = sem("waits_passed")

        SEL_CHAIN = 13

        def slot1(c):
            return 0 if isinstance(c, int) and c == 0 else 2 * c - 1

        def slot2(c):
            return 2 * NCH - 1 if isinstance(c, int) and c == NCH - 1 else 2 * c + 2

        def need(eng, semaphore, value):
            if not isinstance(value, int) or value > 0:
                eng.wait_ge(semaphore, value)

        def need_apart(eng, semaphore, value):
            if not isinstance(value, int) or value > 0:
                eng.wait_ge(semaphore, value).then_inc(waits_passed, 1)

        def walk(eng, do):
            def ffn(slot, parity, first_bank):
                def step(m):
                    if "ffn_step" in do:
                        do["ffn_step"](slot, parity, m, (first_bank + m) % 2)
                return step

            def events(table, m, which):
                for name, arg in table[m]:
                    if name in which and name in do:
                        do[name](*which[name], arg)

            def part(names, args):
                return {name: args for name in names}

            OUT = ("ffn_down_end", "ffn_out", "ffn_outT", "ffn_add")
            PREP = ("ffn_stat", "ffn_norm", "ffn_yT", "ffn_hi", "ffn_lo", "ffn_route", "ffn_exp", "ffn_sel",
                    "ffn_wT", "ffn_wT_copy")

            def slot_x(n):
                known = isinstance(n, int)
                here = not known or n < NCH
                which = {}
                if not known or n >= 2:
                    which |= part(OUT, (slot2(n - 2), 0, 2, n - 2))
                if (not known or n >= 1) and not (known and n > NCH):
                    which |= part([e for m in X_TABLE for e, _ in m if e.startswith("att")], (n - 1,))
                    last = known and n == NCH
                    which |= part(PREP, (slot2(n - 1), 1 if last else 0, 2, n - 1))
                slot, parity = slot1(n), 0 if known and n == 0 else 1
                step = ffn(slot, parity, parity)
                for m in range(STEPS):
                    if here:
                        step(m)
                    events(X_TABLE, m, which)

            def slot_y(n):
                known = isinstance(n, int)
                here = not known or n >= 1
                which = {}
                if not known or n < NCH:
                    which |= part(OUT, (slot1(n), 0 if known and n == 0 else 1, 1, n))
                    which |= part([e for m in Y_TABLE for e, _ in m if e.startswith("att")], (n,))
                if not known or n + 1 < NCH:
                    which |= part(PREP, (slot1(n + 1), 1, 1, n + 1))
                    which |= part(["x_copy"], (n + 1,))
                    which |= part(["x_load"], (n + 1,))
                last = known and n == NCH
                slot, parity = slot2(n - 1), 1 if last else 0
                step = ffn(slot, parity, parity)
                for m in range(STEPS):
                    if here:
                        step(m)
                    events(Y_TABLE, m, which)

            for name in ("x_load", "x_copy"):
                if name in do:
                    do[name](0, 0)
            for name in PREP:
                if name in do:
                    do[name](slot1(0), 0, 1, 0, 0)
            slot_x(0)
            slot_y(0)
            slot_x(1)
            slot_y(1)
            slot_x(2)
            with eng.Fori(2, NCH - 1) as n:
                slot_y(n)
                slot_x(n + 1)
            slot_y(NCH - 1)
            slot_x(NCH)
            slot_y(NCH)
            slot_x(NCH + 1)

        block = ctx.enter_context(nc.Block())

        @block.sync
        def _(sp):
            sp.dma_start(x_next[:], x_dram[0]).then_inc(x_loaded, 16)
            for dst, src in ((wr_raw[:], Wr), (wkv_in[:, 0:KV], Wk), (wkv_in[:, KV:2 * KV], Wv), (wc_in[:], Wc),
                             (we_in[:], We), (bkv_col[:, 0:1], bk.rearrange("(p a) -> p a", a=1)),
                             (bkv_col[:, 1:2], bv.rearrange("(p a) -> p a", a=1)),
                             (wqkv_raw[:, 0:D], Wq), (wo_raw[:], Wo),
                             (bias_raw[:, 0:D], bq.rearrange("(a d) -> a d", a=1)),
                             (bias_raw[:, QKV:QKV + D], bo.rearrange("(a d) -> a d", a=1)),
                             (gamma_b[:], gamma.rearrange("(a d) -> a d", a=1).to_broadcast([P, D])),
                             (beta_b[:], beta.rearrange("(a d) -> a d", a=1).to_broadcast([P, D])),
                             (ebias_b[:], expert_bias.rearrange("(a d) -> a d", a=1).to_broadcast([P, E]))):
                sp.dma_start(dst, src).then_inc(small_loaded, 16)
            sp.dma_start(wd[:, 0:STEPS - 1, :],
                         Wd.rearrange("e f d -> (e f) d").rearrange("(m p) d -> p m d", p=P)).then_inc(w_loaded, 16)
            sp.dma_start(wd[0:FS, STEPS - 1, :], Wd_s).then_inc(w_loaded, 16)

            def x_load(c, _):
                if isinstance(c, int) and c == 0:
                    return
                need_apart(sp, x_copied, c)
                need_apart(sp, norm_made["F"], slot1(c - 1) + 1)
                sp.dma_start(x_next[:], x_dram[c]).then_inc(x_loaded, 16)

            def store(slot, parity, which, c, _):
                if which == 2:
                    need_apart(sp, out_added, slot + 1)
                    sp.dma_start(out_dram[c], y_out[:]).then_inc(out_stored, 16)

            walk(sp, {"x_load": x_load, "ffn_add": store})
            sp.wait_ge(out_stored, 16 * NCH)

        @block.gpsimd
        def _(pool):
            pool.memset(ident[:], 0.0)
            pool.memset(ones[:], 1.0)
            pool.memset(spread_raw[:], 0.0)
            pool.memset(neg_half[:], -0.5).then_inc(zeroed, 1)
            pool.wait_ge(zeroed, 1)
            pool.affine_select(out=ident[:], in_=ident[:], compare_op=ALU.not_equal, fill=1.0, base=0,
                               pattern=[[-1, P]], channel_multiplier=1)
            pool.affine_select(out=tri[:], in_=ones[:], compare_op=ALU.is_ge, fill=0.0, base=0,
                               pattern=[[1, P]], channel_multiplier=-1)
            pool.affine_select(out=spread_raw[:], in_=spread_raw[:], compare_op=ALU.not_equal, fill=1.0, base=0,
                               pattern=[[-1, E], [0, FE]], channel_multiplier=1).then_inc(zeroed, 1)
            pool.wait_ge(zeroed, 2)
            pool.affine_select(out=spread_raw[:], in_=spread_raw[:], compare_op=ALU.not_equal, fill=1.0, base=-E,
                               pattern=[[-1, E], [0, FE]], channel_multiplier=1).then_inc(masks_made, 1)

            def normalise(k, slot, source, free):
                need_apart(pool, moments_made[k], slot + 1)
                pool.tensor_scalar(var_eps[k][:], moments[k][:, :, 1], 1.0, LN_EPS, ALU.mult, ALU.add)
                pool.tensor_scalar(neg_mean[k][:], moments[k][:, :, 0], -1.0, 0.0, ALU.mult, ALU.add
                                   ).then_inc(eps_added[k], 1)
                need(pool, eps_added[k], slot + 1)
                pool.tensor_tensor(rstd[k][:], var_eps[k][:], neg_half[:], ALU.pow).then_inc(rstd_made[k], 1)
                free()
                need_apart(pool, rstd_made[k], slot + 1)
                for i in range(TILES):
                    last = pool.tensor_scalar(normed[k][:, i, :], source[:, i, :], neg_mean[k][:, i:i + 1],
                                              rstd[k][:, i:i + 1], ALU.add, ALU.mult)
                last.then_inc(norm_made[k], 1)

            def ffn_norm(slot, parity, which, c, _):
                def free():
                    need(pool, fyT_ready, slot)
                normalise("F", slot, x_next if which == 1 else x2, free)

            def att_norm(c, _):
                def free():
                    need(pool, z_added, c)
                normalise("A", c, x1, free)
                need(pool, x2_made, c)
                pool.tensor_tensor(x1_beta[:], x1[:], broadcast_free(beta_b[:], 1, TILES), ALU.add
                                   ).then_inc(beta_added, 1)

            def att_norm_z(c, _):
                def free():
                    need(pool, z_scaled, c)
                normalise("Z", c, att_z, free)

            def att_kv(c, i):
                need(pool, feat_made, 2 * c + i // 2 + 1)
                if i == 0:
                    need(pool, cum_ready, TILES * c)
                key = qk_feat[:, i, D:D + KV].rearrange("p (g f) -> p g f", g=G)
                pool.tensor_tensor(kv[:, i, :].rearrange("p (g f v) -> p g f v", g=G, f=HD),
                                   broadcast_free(key, 3, V1), broadcast_free(v_ones[:, i], 2, HD), ALU.mult
                                   ).then_inc(kv_made, 1)

            def att_mul(c, i):
                need(pool, cum_copied, TILES * c + i + 1)
                need(pool, red_made, TILES * c + i - 1)
                for g in range(G):
                    qf = qk_feat[:, i, g * R * HD:(g + 1) * R * HD].rearrange("p (r f) -> p r f", r=R)
                    cum = kv_cum[:, i % 2, g * HD * V1:(g + 1) * HD * V1].rearrange("p (f v) -> p f v", f=HD)
                    dst = prod[:, i % 2, g * R * HD * V1:(g + 1) * R * HD * V1]
                    last = pool.tensor_tensor(dst.rearrange("p (r f v) -> p r f v", r=R, f=HD),
                                              broadcast_free(qf, 3, V1), broadcast_free(cum, 1, R), ALU.mult)
                last.then_inc(prod_made, 1)

            walk(pool, {"ffn_norm": ffn_norm, "att_norm": att_norm, "att_norm_z": att_norm_z,
                        "att_kv": att_kv, "att_mul": att_mul})

        @block.scalar
        def _(act):
            act.dma_start(wg_raw[:, 0:FR].rearrange("p (e f) -> p e f", e=E), Wg.rearrange("e d f -> d e f")
                          ).then_inc(w_loaded, 16)
            act.dma_start(wu_raw[:, 0:FR].rearrange("p (e f) -> p e f", e=E), Wu.rearrange("e d f -> d e f")
                          ).then_inc(w_loaded, 16)
            act.dma_start(wg_raw[:, FR:FR + FS], Wg_s).then_inc(w_loaded, 16)
            act.dma_start(wu_raw[:, FR:FR + FS], Wu_s).then_inc(w_loaded, 16)
            act.wait_ge(small_loaded, 16 * 14)
            act.copy(wr_hi[:], wr_raw[:]).then_inc(hi_made, 1)
            act.wait_ge(w_loaded, 16 * 6)
            act.copy(wg_hi[:], wg_raw[:]).then_inc(hi_made, 1)
            act.copy(wu_hi[:], wu_raw[:]).then_inc(hi_made, 1)
            act.wait_ge(fold_copied, 4)
            act.copy(wqkv_hi[:], wqkv_raw[:]).then_inc(hi_made, 1)
            act.copy(wo_hi[:], wo_raw[:]).then_inc(hi_made, 1)
            act.copy(bias_hi[:], bias_raw[:]).then_inc(hi_made, 1)

            def x_copy(c, _):
                need(act, x_loaded, 16 * (c + 1))
                need(act, out_added, slot1(c - 1) + 1 if not (isinstance(c, int) and c == 0) else 0)
                act.copy(x_cur[:], x_next[:]).then_inc(x_copied, 1)

            def ffn_hi(slot, parity, which, c, _):
                need(act, fyT_ready, slot + 1)
                act.copy(fyT_hi[parity][:], ps_f[:]).then_inc(fyT_hi_made, 1)

            def ffn_exp(slot, parity, which, c, _):
                need(act, logits_ready, slot + 1)
                need(act, w_made, slot)
                act.activation(exp_neg[:], ps_f[:, 0:TILES * E].rearrange("p (i e) -> p i e", e=E), ACT.Exp,
                               scale=-1.0).then_inc(exp_made, 1)

            def ffn_wT_copy(slot, parity, which, c, _):
                need(act, wT_ready, slot + 1)
                act.copy(wT[parity][:], ps_f[0:2 * E, :]).then_inc(wT_copied, 1)

            def ffn_step(slot, parity, m, b):
                rows = P if m < STEPS - 1 else FS
                need(act, gate_ready, STEPS * slot + m + 1)
                need(act, hidden_made, STEPS * slot + m - 1)
                act.activation(silu_g[b][0:rows, :], ps_gate[b][0:rows, :], ACT.Silu).then_inc(silu_made, 1)

            def ffn_out(slot, parity, which, c, _):
                need(act, down_ready, slot + 1)
                need(act, out_ready, slot)
                act.copy(downT[:], ps_down[:]).then_inc(down_copied, 1)

            def att_hi(c, _):
                need(act, ayT_ready, c + 1)
                act.copy(ayT_hi[:], ps_a[:]).then_inc(ayT_hi_made, 1)

            def att_exp(c, j):
                t = slice(2 * j, 2 * j + 2)
                need(act, qkv_ready, 2 * c + j + 1)
                if j == 0:
                    need(act, feat_made, 2 * c)
                    need(act, kv_made, TILES * c)
                src = ps_a[:, 0:2 * QKV].rearrange("p (i q) -> p i q", i=2)
                act.activation(qk_exp[:, t, :], src[:, :, 0:D + KV], ACT.Exp)
                act.activation(qk_relu[:, t, :], src[:, :, 0:D + KV], ACT.Relu)
                for i in range(2):
                    last = act.copy(v_ones[:, 2 * j + i, :, 0:HD],
                                    src[:, i, D + KV:QKV].rearrange("p (g v) -> p g v", g=G))
                last.then_inc(qkv_read, 1)

            def att_cum_copy(c, i):
                need(act, cum_ready, TILES * c + i + 1)
                need(act, prod_made, TILES * c + i - 1)
                act.copy(kv_cum[:, i % 2, :], ps_a[:, 0:KVC]).then_inc(cum_copied, 1)

            def att_o_hi(c, _):
                need(act, oT_ready, c + 1)
                act.copy(oT_hi[:], ps_a[:]).then_inc(oT_hi_made, 1)

            walk(act, {"x_copy": x_copy, "ffn_hi": ffn_hi, "ffn_exp": ffn_exp, "ffn_wT_copy": ffn_wT_copy,
                       "ffn_step": ffn_step, "ffn_out": ffn_out, "att_hi": att_hi, "att_exp": att_exp,
                       "att_cum_copy": att_cum_copy, "att_o_hi": att_o_hi})

        @block.vector
        def _(dve):
            dve.memset(v_ones[:], 1.0).then_inc(dve_consts, 1)
            for e in range(E):
                last = dve.memset(iota_e[:, e:e + 1], float(e))
            last.then_inc(dve_consts, 1)
            dve.wait_ge(masks_made, 1)
            dve.tensor_copy(spread[:], spread_raw[:])
            dve.tensor_copy(ones_row[:], ones[0:1, :]).then_inc(consts_made, 1)
            dve.wait_ge(fold_ready, 1)
            dve.tensor_copy(wcT[:], ps_a[0:L, 0:KV])
            dve.tensor_copy(wkvT[:], ps_a[0:KV, P:3 * P].rearrange("p (a b) -> p a b", a=2)).then_inc(fold_copied, 1)
            dve.wait_ge(fold_ready, 2)
            dve.tensor_copy(wce[:], ps_a[0:KV, 0:KV]).then_inc(fold_copied, 1)
            dve.wait_ge(fold_ready, 3)
            dve.tensor_copy(wqkv_raw[:, D:QKV], ps_a[:, 0:2 * KV])
            dve.wait_ge(small_loaded, 16 * 14)
            dve.tensor_copy(bias_raw[:, D:QKV], ps_a[0:1, 2 * KV:4 * KV]).then_inc(fold_copied, 2)
            dve.wait_ge(fold_copied, 4)
            for n, (lo, hi, raw) in enumerate(((wr_lo, wr_hi, wr_raw), (wg_lo, wg_hi, wg_raw),
                                               (wu_lo, wu_hi, wu_raw), (wqkv_lo, wqkv_hi, wqkv_raw),
                                               (wo_lo, wo_hi, wo_raw), (bias_lo, bias_hi, bias_raw))):
                dve.wait_ge(hi_made, n + 1)
                dve.tensor_tensor(lo[:], raw[:], hi[:].bitcast(F32), ALU.subtract).then_inc(weights_split, 1)

            def statistics(k, slot, source):
                for i in range(TILES):
                    last = dve.bn_stats(stats[k][:, i, :], source[:, i, :])
                last.then_inc(stats_made[k], 1)
                need(dve, stats_made[k], slot + 1)
                need_apart(dve, norm_made[k], slot)
                for i in range(TILES):
                    last = dve.bn_aggr(moments[k][:, i, :], stats[k][:, i, :])
                last.then_inc(moments_made[k], 1)

            def ffn_stat(slot, parity, which, c, _):
                if which == 1:
                    need(dve, x_loaded, 16 * (c + 1))
                    statistics("F", slot, x_next)
                else:
                    need(dve, x2_made, c + 1)
                    statistics("F", slot, x2)

            def ffn_lo(slot, parity, which, c, _):
                need(dve, fyT_hi_made, slot + 1)
                dve.tensor_tensor(fyT_lo[parity][:], ps_f[:], fyT_hi[parity][:].bitcast(F32), ALU.subtract
                                  ).then_inc(fyT_lo_made, 1)

            def ffn_sel(slot, parity, which, c, _):
                base = SEL_CHAIN * slot
                done = [0]

                def link(ins):
                    done[0] += 1
                    ins.then_inc(sel_chain, 1)
                    need_apart(dve, sel_chain, base + done[0])

                need(dve, exp_made, slot + 1)
                need(dve, wT_ready, slot)
                link(dve.tensor_scalar(denom[:], exp_neg[:], 1.0, None, ALU.add))
                link(dve.reciprocal(score[:], denom[:]))
                link(dve.tensor_tensor(biased[:], score[:], broadcast_free(ebias_b[:], 1, TILES), ALU.add))
                for i in range(TILES):
                    last = dve.max(top_val[:, i, :], biased[:, i, :])
                link(last)
                for i in range(TILES):
                    last = dve.max_index(top_idx[:, i, :], top_val[:, i, :], biased[:, i, :])
                link(last)
                iota = broadcast_free(iota_e[:], 1, TILES)
                dve.tensor_tensor(is_first[:], iota, top_idx[:, :, 0:1].to_broadcast([P, TILES, E]), ALU.is_equal)
                link(dve.tensor_tensor(is_second[:], iota, top_idx[:, :, 1:2].to_broadcast([P, TILES, E]),
                                       ALU.is_equal))
                link(dve.tensor_tensor(chosen[:], is_first[:], is_second[:], ALU.add))
                link(dve.tensor_tensor(picked[:], score[:], chosen[:], ALU.mult))
                link(dve.tensor_reduce(pick_sum[:], picked[:], AX_X, ALU.add))
                link(dve.tensor_scalar(pick_sum_eps[:], pick_sum[:], ROUTE_EPS, None, ALU.add))
                link(dve.reciprocal(pick_inv[:], pick_sum_eps[:]))
                link(dve.tensor_tensor(route_w[:], picked[:], broadcast_free(pick_inv[:], 2, E), ALU.mult))
                link(dve.tensor_copy(route_parts[:, :, 0:E], route_w[:]))
                assert done[0] == SEL_CHAIN
                dve.tensor_tensor(route_parts[:, :, E:2 * E], route_w[:], route_parts[:, :, 0:E].bitcast(F32),
                                  ALU.subtract).then_inc(w_made, 1)

            def ffn_step(slot, parity, m, b):
                routed = m < STEPS - 1
                rows = P if routed else FS
                need(dve, silu_made, STEPS * slot + m + 1)
                need(dve, up_ready, STEPS * slot + m + 1)
                if routed:
                    dve.tensor_tensor(gated[b][:], silu_g[b][:], ps_up[b][:], ALU.mult).then_inc(gated_made, 1)
                    need(dve, gated_made, (STEPS - 1) * slot + m + 1)
                    dve.tensor_tensor(hidden[:, m, :], gated[b][:], ps_w[:], ALU.mult).then_inc(hidden_made, 1)
                else:
                    dve.tensor_tensor(hidden[0:rows, m, :], silu_g[b][0:rows, :], ps_up[b][0:rows, :], ALU.mult
                                      ).then_inc(hidden_made, 1)

            def ffn_add(slot, parity, which, c, _):
                need(dve, out_ready, slot + 1)
                if which == 1:
                    need(dve, x_copied, c + 1)
                    need(dve, beta_added, c)
                    src, dst = x_cur, x1
                else:
                    need(dve, out_stored, 16 * c)
                    src, dst = x2, y_out
                dve.scalar_tensor_tensor(out=dst[:], in0=ps_f[:].rearrange("p (i d) -> p i d", i=TILES), scalar=0.5,
                                         in1=src[:], op0=ALU.mult, op1=ALU.add).then_inc(out_added, 1)

            def att_stat(c, _):
                need(dve, out_added, slot1(c) + 1)
                statistics("A", c, x1)

            def att_lo(c, _):
                need(dve, ayT_hi_made, c + 1)
                dve.tensor_tensor(ayT_lo[:], ps_a[:], ayT_hi[:].bitcast(F32), ALU.subtract).then_inc(ayT_lo_made, 1)

            def att_feat(c, j):
                t = slice(2 * j, 2 * j + 2)
                need(dve, qkv_read, 2 * c + j + 1)
                if j == 0:
                    need(dve, prod_made, TILES * c)
                dve.scalar_tensor_tensor(out=qk_feat[:, t, :], in0=qk_exp[:, t, :], scalar=1.0,
                                         in1=qk_relu[:, t, :], op0=ALU.min, op1=ALU.add).then_inc(feat_made, 1)

            def att_red(c, i):
                need(dve, prod_made, TILES * c + i + 1)
                dve.tensor_reduce(num_den[:, i], prod[:, i % 2, :].rearrange("p (h f v) -> p h v f", h=H, f=HD),
                                  AX_X, ALU.add).then_inc(red_made, 1)

            def att_div(c, _):
                need(dve, red_made, TILES * (c + 1))
                dve.tensor_scalar(den_eps[:], num_den[:, :, :, HD], DEN_EPS, None, ALU.add).then_inc(den_chain, 1)
                need(dve, den_chain, 2 * c + 1)
                dve.reciprocal(den_inv[:], den_eps[:]).then_inc(den_chain, 1)
                need(dve, den_chain, 2 * c + 2)
                need(dve, oT_ready, c)
                dve.tensor_tensor(att_o[:].rearrange("p i (h v) -> p i h v", h=H), num_den[:, :, :, 0:HD],
                                  broadcast_free(den_inv[:], 3, HD), ALU.mult).then_inc(o_made, 1)

            def att_o_lo(c, _):
                need(dve, oT_hi_made, c + 1)
                dve.tensor_tensor(oT_lo[:], ps_a[:], oT_hi[:].bitcast(F32), ALU.subtract).then_inc(oT_lo_made, 1)

            def att_res(c, _):
                need(dve, z_ready, c + 1)
                need(dve, norm_made["Z"], c)
                dve.tensor_tensor(att_z[:], ps_a[:].rearrange("p (i d) -> p i d", i=TILES), normed["A"][:], ALU.add
                                  ).then_inc(z_added, 1)
                need(dve, z_added, c + 1)
                statistics("Z", c, att_z)

            def att_x2(c, _):
                need(dve, norm_made["Z"], c + 1)
                dve.tensor_tensor(z_gamma[:], normed["Z"][:], broadcast_free(gamma_b[:], 1, TILES), ALU.mult
                                  ).then_inc(z_scaled, 1)
                need(dve, z_scaled, c + 1)
                need(dve, beta_added, c + 1)
                dve.tensor_tensor(x2[:], z_gamma[:], x1_beta[:], ALU.add).then_inc(x2_made, 1)

            walk(dve, {"ffn_stat": ffn_stat, "ffn_lo": ffn_lo, "ffn_sel": ffn_sel, "ffn_step": ffn_step,
                       "ffn_add": ffn_add, "att_stat": att_stat, "att_lo": att_lo, "att_feat": att_feat,
                       "att_red": att_red, "att_div": att_div, "att_o_lo": att_o_lo, "att_res": att_res,
                       "att_x2": att_x2})

        @block.tensor
        def _(pe):
            pe.wait_ge(masks_made, 1)
            pe.wait_ge(small_loaded, 16 * 14)
            pe.transpose(ps_a[0:L, 0:KV], wc_in[:], ident[0:KV, 0:KV])
            for j in range(2):
                last = pe.transpose(ps_a[0:KV, (1 + j) * P:(2 + j) * P], wkv_in[:, j * KV:(j + 1) * KV], ident[:])
            last.then_inc(fold_ready, 1)
            pe.wait_ge(fold_copied, 1)
            pe.matmul(ps_a[0:KV, 0:KV], wcT[:], we_in[:], start=True, stop=True).then_inc(fold_ready, 1)
            pe.wait_ge(fold_copied, 2)
            for j in range(2):
                pe.matmul(ps_a[:, j * KV:(j + 1) * KV], wkvT[:, j, :], wce[:], start=True, stop=True)
            for j in range(2):
                last = pe.matmul(ps_a[0:1, (2 + j) * KV:(3 + j) * KV], bkv_col[:, j:j + 1], wce[:],
                                 start=True, stop=True)
            last.then_inc(fold_ready, 1)
            pe.wait_ge(weights_split, 6)
            pe.wait_ge(consts_made, 1)
            pe.wait_ge(w_loaded, 16 * 6)

            def ffn_yT(slot, parity, which, c, _):
                need(pe, norm_made["F"], slot + 1)
                outs = 2 * NCH - 1 if isinstance(slot, int) and slot == 2 * NCH - 1 else slot - 1
                need(pe, out_added, outs)
                for i in range(TILES):
                    last = pe.transpose(ps_f[:, i * P:(i + 1) * P], normed["F"][:, i, :], ident[:])
                last.then_inc(fyT_ready, 1)

            def ffn_route(slot, parity, which, c, _):
                need(pe, fyT_lo_made, slot + 1)
                for i in range(TILES):
                    dst, t = ps_f[:, i * E:(i + 1) * E], slice(i * P, (i + 1) * P)
                    pe.matmul(dst, fyT_hi[parity][:, t], wr_hi[:], start=True, stop=False)
                    pe.matmul(dst, fyT_hi[parity][:, t], wr_lo[:], start=False, stop=False)
                    last = pe.matmul(dst, fyT_lo[parity][:, t], wr_hi[:], start=False, stop=True)
                last.then_inc(logits_ready, 1)

            def ffn_wT(slot, parity, which, c, _):
                need(pe, w_made, slot + 1)
                for i in range(TILES):
                    last = pe.transpose(ps_f[0:2 * E, i * P:(i + 1) * P], route_parts[:, i, :].bitcast(F32), ident[:])
                last.then_inc(wT_ready, 1)

            def down(slot, m):
                rows = P if m < STEPS - 1 else FS
                need(pe, hidden_made, STEPS * slot + m + 1)
                if m == 0:
                    need(pe, down_copied, slot)
                last = pe.matmul(ps_down[:], wd[0:rows, m, :], hidden[0:rows, m, :], start=(m == 0),
                                 stop=(m == STEPS - 1))
                if m == STEPS - 1:
                    last.then_inc(down_ready, 1)

            def split_matmul(dst, w_hi, w_lo, y_hi, y_lo):
                pe.matmul(dst, w_hi, y_hi, start=True, stop=False)
                pe.matmul(dst, w_hi, y_lo, start=False, stop=False)
                return pe.matmul(dst, w_lo, y_hi, start=False, stop=True)

            def ffn_step(slot, parity, m, b):
                routed = m < STEPS - 1
                rows = P if routed else FS
                f = slice(m * P, m * P + rows)
                t = STEPS * slot + m
                if m == 0:
                    need(pe, wT_copied, slot + 1)
                need(pe, silu_made, t - 1)
                split_matmul(ps_gate[b][0:rows, :], wg_hi[:, f], wg_lo[:, f], fyT_hi[parity][:], fyT_lo[parity][:]
                             ).then_inc(gate_ready, 1)
                need(pe, hidden_made, t - 1)
                last = split_matmul(ps_up[b][0:rows, :], wu_hi[:, f], wu_lo[:, f], fyT_hi[parity][:],
                                    fyT_lo[parity][:])
                if routed:
                    need(pe, hidden_made, t)
                    last = pe.matmul(ps_w[:], spread[:, f], wT[parity][:], start=True, stop=True)
                last.then_inc(up_ready, 1)
                if m >= 2:
                    down(slot, m - 2)

            def ffn_down_end(slot, parity, which, c, _):
                down(slot, STEPS - 2)
                down(slot, STEPS - 1)

            def ffn_outT(slot, parity, which, c, _):
                need(pe, down_copied, slot + 1)
                need(pe, wT_copied, slot + 1)
                for i in range(TILES):
                    last = pe.transpose(ps_f[:, i * P:(i + 1) * P], downT[:, i * P:(i + 1) * P], ident[:])
                last.then_inc(out_ready, 1)

            def att_yT(c, _):
                need(pe, norm_made["A"], c + 1)
                need(pe, z_added, c)
                for i in range(TILES):
                    last = pe.transpose(ps_a[:, i * P:(i + 1) * P], normed["A"][:, i, :], ident[:])
                last.then_inc(ayT_ready, 1)

            def bias_and_split(dst, y_hi, y_lo, w_hi, w_lo, cols):
                pe.matmul(dst, ones_row[:], bias_hi[:, cols], start=True, stop=False)
                pe.matmul(dst, ones_row[:], bias_lo[:, cols], start=False, stop=False)
                pe.matmul(dst, y_hi, w_hi[:], start=False, stop=False)
                pe.matmul(dst, y_hi, w_lo[:], start=False, stop=False)
                return pe.matmul(dst, y_lo, w_hi[:], start=False, stop=True)

            def att_qkv(c, j):
                if j == 0:
                    need(pe, ayT_lo_made, c + 1)
                else:
                    need(pe, qkv_read, 2 * c + 1)
                for i in range(2):
                    t = slice((2 * j + i) * P, (2 * j + i + 1) * P)
                    last = bias_and_split(ps_a[:, i * QKV:(i + 1) * QKV], ayT_hi[:, t], ayT_lo[:, t],
                                          wqkv_hi, wqkv_lo, slice(0, QKV))
                last.then_inc(qkv_ready, 1)

            def att_cum(c, i):
                need(pe, kv_made, TILES * c + i + 1)
                if i == 0:
                    need(pe, qkv_read, 2 * c + 2)
                else:
                    need(pe, cum_copied, TILES * c + i)
                if i % 2:
                    pe.matmul(ps_a[:, 0:KVC], ones[:], kv[:, i - 1, :], start=True, stop=False)
                pe.matmul(ps_a[:, 0:KVC], tri[:], kv[:, i, :], start=(i % 2 == 0), stop=True).then_inc(cum_ready, 1)

            def att_oT(c, _):
                need(pe, o_made, c + 1)
                need(pe, cum_copied, TILES * (c + 1))
                for i in range(TILES):
                    last = pe.transpose(ps_a[:, i * P:(i + 1) * P], att_o[:, i, :], ident[:])
                last.then_inc(oT_ready, 1)

            def att_proj(c, _):
                need(pe, oT_lo_made, c + 1)
                for i in range(TILES):
                    t = slice(i * P, (i + 1) * P)
                    last = bias_and_split(ps_a[:, t], oT_hi[:, t], oT_lo[:, t], wo_hi, wo_lo, slice(QKV, QKV + D))
                last.then_inc(z_ready, 1)

            walk(pe, {"ffn_yT": ffn_yT, "ffn_route": ffn_route, "ffn_wT": ffn_wT, "ffn_step": ffn_step,
                      "ffn_down_end": ffn_down_end, "ffn_outT": ffn_outT, "att_yT": att_yT, "att_qkv": att_qkv,
                      "att_cum": att_cum, "att_oT": att_oT, "att_proj": att_proj})


_INS = ["L0_attn_x", "L0_attn_Wq", "L0_attn_bq", "L0_attn_Wk", "L0_attn_bk", "L0_attn_Wv", "L0_attn_bv",
        "L0_attn_Wc", "L0_attn_We", "L0_attn_Wo", "L0_attn_bo", "L0_attn_gamma", "L0_attn_beta",
        "L0_ffn_W_gate_router", "L0_ffn_expert_bias", "L0_ffn_Wg", "L0_ffn_Wu", "L0_ffn_Wd",
        "L0_ffn_Wg_s", "L0_ffn_Wu_s", "L0_ffn_Wd_s"]


def kernel(**inputs):
    import numpy as _np
    import concourse.bacc as _bacc
    from concourse import mybir as _mybir
    from concourse.bass_utils import run_bass_kernel_spmd as _run

    nc = _bacc.Bacc("TRN2", target_bir_lowering=False, num_devices=1)
    arrays, args = {}, []
    for name in _INS:
        a = _np.ascontiguousarray(inputs[name])
        arrays[f"in_{name}"] = a
        args.append(nc.dram_tensor(f"in_{name}", a.shape, _mybir.dt.from_np(a.dtype), kind="ExternalInput").ap())
    shape = inputs["L0_attn_x"].shape
    args.append(nc.dram_tensor("out_0", shape, _mybir.dt.float32, kind="ExternalOutput").ap())
    macaron_kernel(nc, *args)
    r = _run(nc, [arrays], core_ids=[0])
    return r.results[0]["out_0"]
```

```python
from contextlib import ExitStack

import concourse.bass as bass
from concourse import mybir

ALU = mybir.AluOpType
ACT = mybir.ActivationFunctionType
F32 = mybir.dt.float32
F32R = mybir.dt.float32r
U32 = mybir.dt.uint32
AX_X = mybir.AxisListType.X

P = 128
LN_EPS = 1e-5
DEN_EPS = 1e-6
ROUTE_EPS = 1e-20
TILES = 4
CHUNK = TILES * P
STEPS = 7

START_TABLE = [
    ["in_stat", "in_aggr", "start_fold:0", "start_ffn:0", "start_route", "start_consts", "in_norm", "in_yT",
     "start_fold:1", "in_hi", "in_lo", "in_route", "in_sel:0", "in_sel:1", "in_sel:2", "start_fold:2", "in_sel:3",
     "start_ffn:1", "in_sel:4", "in_sel:5", "in_sel:6", "in_sel:7", "in_exp", "in_sel:8", "in_sel:9", "in_sel:10",
     "start_att"],
]
FIRST_TABLE = [
    ["out_down", "out_copy", "ffn_up", "ffn_gated", "now_sel:11", "now_sel:12", "now_sel:13", "ffn_hidden",
     "now_sel:14", "now_wT", "now_wT_copy"],
    ["ffn_up", "ffn_gated", "ffn_w", "ffn_hidden", "out_T", "out_add", "x_copy"],
    ["att_stat", "ffn_down", "att_aggr", "ffn_up", "ffn_gated", "ffn_w", "ffn_hidden", "att_norm"],
    ["ffn_down", "ffn_w", "ffn_up", "ffn_gated", "ffn_hidden", "att_yT", "att_hi", "att_lo", "in_stat"],
    ["ffn_down", "in_aggr", "in_norm", "ffn_up", "ffn_w", "ffn_gated", "ffn_hidden", "att_qkv:0", "att_qkv:1",
     "att_exp:0", "att_feat:0", "att_kv:0", "att_kv:1", "att_exp:1", "att_feat:1", "att_kv:2", "att_kv:3", "in_yT",
     "in_hi", "in_lo"],
    ["ffn_up", "ffn_gated", "ffn_w", "in_route", "in_exp", "ffn_down", "ffn_hidden", "in_sel:0", "in_sel:1",
     "in_sel:2", "in_sel:3"],
    ["in_sel:4", "in_sel:5", "ffn_up", "ffn_gated", "in_sel:6", "ffn_w", "ffn_down", "in_sel:7", "in_sel:8",
     "in_sel:9", "ffn_hidden", "in_sel:10"],
]
RAMP_TABLE = [
    ["ffn_up", "ffn_gated", "out_down", "now_sel:11", "now_sel:12", "now_sel:13", "ffn_hidden", "now_sel:14",
     "now_wT", "now_wT_copy", "out_copy"],
    ["prev_cum:0", "prev_cum_copy:0", "ffn_up", "ffn_gated", "prev_mul:0", "ffn_w", "ffn_hidden", "prev_red:0"],
    ["prev_cum:1", "prev_cum_copy:1", "prev_cum_copy:2", "ffn_up", "ffn_gated", "ffn_down", "prev_cum:2", "ffn_w",
     "ffn_hidden"],
    ["prev_mul:1", "prev_red:1", "ffn_up", "ffn_gated", "ffn_down", "ffn_w", "ffn_hidden", "prev_cum:3",
     "prev_cum_copy:3", "prev_mul:2", "prev_red:2"],
    ["prev_mul:3", "ffn_up", "ffn_gated", "ffn_w", "ffn_hidden", "prev_red:3", "end_div:0", "prev_beta",
     "end_div:1", "ffn_down", "end_div:2", "end_oT", "end_o_hi", "out_T", "out_add", "x_copy"],
    ["end_o_lo", "ffn_up", "ffn_w", "ffn_gated", "ffn_down", "ffn_hidden", "end_proj", "end_res", "att_stat",
     "end_stat", "att_aggr", "att_norm", "end_aggr"],
    ["ffn_up", "ffn_gated", "ffn_w", "ffn_hidden", "att_yT", "ffn_down", "att_hi", "att_lo", "att_qkv:0",
     "att_exp:0", "end_norm", "att_feat:0", "att_qkv:1", "att_exp:1", "att_feat:1", "end_zg", "x2_copy", "att_kv:0",
     "att_kv:1", "att_kv:2", "end_x2", "att_kv:3", "att_cum:0", "att_cum_copy:0", "in_stat", "att_cum:1",
     "att_cum_copy:1", "in_aggr", "in_norm", "att_mul:0", "in_yT", "in_hi", "att_mul:1", "att_cum:2", "in_lo",
     "att_red:0", "att_cum_copy:2", "in_route", "in_exp", "att_mul:2", "att_red:1", "in_sel:0", "att_red:2",
     "in_sel:1", "in_sel:2", "in_sel:3", "in_sel:4", "att_cum:3", "att_cum_copy:3", "att_mul:3", "att_red:3",
     "in_sel:5", "in_sel:6", "in_sel:7", "in_sel:8", "in_sel:9", "in_sel:10", "att_beta"],
]
Y_TABLE = [
    ["ffn_up", "ffn_gated", "out_down", "ffn_hidden", "now_sel:11", "end_div:0", "end_div:1", "now_sel:12",
     "now_sel:13", "now_sel:14", "now_wT", "now_wT_copy", "end_div:2", "end_oT", "end_o_hi", "in_stat", "out_copy"],
    ["ffn_up", "end_o_lo", "in_aggr", "in_norm", "ffn_gated", "end_proj", "out_T", "end_res", "end_stat",
     "end_aggr", "end_norm", "ffn_w", "out_add", "x_copy", "ffn_hidden"],
    ["ffn_up", "att_stat", "ffn_down", "ffn_w", "ffn_gated", "in_yT", "in_hi", "att_aggr", "ffn_hidden"],
    ["in_lo", "end_zg", "ffn_down", "ffn_w", "att_norm", "ffn_up", "ffn_gated", "ffn_hidden", "in_route", "att_yT",
     "att_hi", "end_x2"],
    ["att_lo", "ffn_up", "ffn_down", "ffn_w", "ffn_gated", "in_exp", "ffn_hidden", "att_qkv:0", "att_exp:0",
     "in_sel:0", "in_sel:1", "att_feat:0", "att_qkv:1", "att_exp:1", "att_kv:0", "in_sel:2", "in_sel:3",
     "att_feat:1"],
    ["in_sel:4", "ffn_up", "ffn_gated", "ffn_down", "att_kv:1", "att_kv:2", "ffn_w", "ffn_hidden", "in_sel:5",
     "in_sel:6", "att_kv:3"],
    ["ffn_up", "in_sel:7", "ffn_gated", "in_sel:8", "ffn_down", "ffn_w", "ffn_hidden", "in_sel:9", "in_sel:10"],
]
X_TABLE = [
    ["ffn_up", "ffn_gated", "out_down", "out_copy", "now_sel:11", "now_sel:12", "now_sel:13", "now_sel:14",
     "now_wT", "att_cum:0", "att_cum_copy:0", "now_wT_copy", "ffn_hidden", "in_stat"],
    ["ffn_up", "in_aggr", "in_norm", "att_mul:0", "out_T", "ffn_gated", "att_cum:1", "out_add", "ffn_w",
     "ffn_hidden"],
    ["ffn_up", "ffn_gated", "out_store", "ffn_down", "ffn_w", "att_cum_copy:1", "att_mul:1", "in_yT", "in_hi",
     "ffn_hidden"],
    ["att_cum:2", "x2_copy", "ffn_up", "ffn_down", "att_red:0", "ffn_w", "in_lo", "att_cum_copy:2", "att_mul:2",
     "ffn_gated", "ffn_hidden", "att_cum:3", "att_red:1", "in_route", "in_exp", "in_sel:0"],
    ["att_cum_copy:3", "in_sel:1", "ffn_up", "ffn_gated", "ffn_down", "ffn_w", "ffn_hidden", "att_mul:3",
     "in_sel:2", "in_sel:3"],
    ["ffn_down", "att_red:2", "in_sel:4", "ffn_up", "ffn_gated", "in_sel:5", "in_sel:6", "ffn_w", "ffn_hidden",
     "att_red:3"],
    ["in_sel:7", "ffn_up", "ffn_w", "att_beta", "ffn_gated", "in_sel:8", "in_sel:9", "ffn_hidden", "ffn_down",
     "in_sel:10"],
]
TAIL_TABLE = [
    ["ffn_up", "ffn_gated", "end_div:0", "ffn_hidden", "now_sel:11", "now_sel:12", "end_div:1", "out_down",
     "out_copy", "now_sel:13", "end_div:2", "now_sel:14", "now_wT", "end_oT"],
    ["ffn_up", "ffn_w", "now_wT_copy", "out_T", "end_o_hi", "end_o_lo", "ffn_gated", "ffn_hidden", "end_proj",
     "end_res", "end_stat"],
    ["end_aggr", "end_norm", "out_add", "ffn_up", "att_stat", "ffn_gated", "ffn_down", "att_aggr", "att_norm",
     "ffn_w", "ffn_hidden"],
    ["end_zg", "end_x2", "ffn_up", "ffn_gated", "ffn_down", "ffn_w", "ffn_hidden", "in_stat", "att_yT", "att_hi",
     "att_lo", "in_aggr", "in_norm"],
    ["ffn_up", "ffn_gated", "att_qkv:0", "ffn_down", "ffn_w", "ffn_hidden", "att_exp:0", "att_qkv:1", "att_exp:1",
     "att_feat:0", "att_kv:0", "att_kv:1", "att_feat:1", "att_kv:2", "att_kv:3", "in_yT", "in_hi", "in_lo"],
    ["ffn_up", "ffn_gated", "ffn_down", "ffn_w", "ffn_hidden", "in_route", "in_exp", "in_sel:0", "in_sel:1"],
    ["in_sel:2", "in_sel:3", "in_sel:4", "ffn_up", "ffn_gated", "ffn_down", "in_sel:5", "in_sel:6", "in_sel:7",
     "ffn_w", "ffn_hidden", "in_sel:8", "in_sel:9", "in_sel:10"],
]
LATE_TABLE = [
    ["ffn_up", "out_down", "att_cum:0", "ffn_gated", "ffn_hidden", "out_copy", "now_sel:11", "now_sel:12"],
    ["now_sel:13", "now_sel:14", "now_wT", "now_wT_copy", "att_cum_copy:0", "ffn_up", "ffn_gated", "ffn_w",
     "ffn_hidden", "att_mul:0", "out_T"],
    ["ffn_down", "out_add", "att_cum:1", "att_cum_copy:1", "ffn_up", "ffn_gated", "att_cum:2", "ffn_w", "ffn_hidden"],
    ["ffn_up", "att_mul:1", "out_store", "att_cum_copy:2", "att_red:0", "ffn_gated", "x2_copy", "ffn_w",
     "att_cum:3", "ffn_down", "ffn_hidden", "att_mul:2", "att_red:1"],
    ["ffn_up", "ffn_gated", "att_red:2", "ffn_down", "ffn_w", "ffn_hidden"],
    ["ffn_down", "ffn_up", "ffn_gated", "ffn_w", "ffn_hidden", "att_cum_copy:3"],
    ["att_mul:3", "att_red:3", "att_beta", "end_div:0", "ffn_w", "ffn_up", "end_div:1", "ffn_gated", "end_div:2",
     "end_oT", "ffn_down", "end_o_hi", "end_o_lo", "end_proj", "end_res", "end_stat", "end_aggr", "end_norm",
     "ffn_hidden", "end_zg", "end_x2", "in_stat", "in_aggr", "in_norm", "in_yT", "in_hi", "in_lo", "in_route",
     "in_exp", "in_sel:0", "in_sel:1", "in_sel:2", "in_sel:3", "in_sel:4", "in_sel:5", "in_sel:6", "in_sel:7",
     "in_sel:8", "in_sel:9", "in_sel:10"],
]

def broadcast_free(ap, axis, n):
    names = [f"a{i}" for i in range(len(ap.shape))]
    new = names[:axis] + ["z"] + names[axis:]
    if axis < len(names):
        joined = names[:axis] + [f"(z {names[axis]})"] + names[axis + 1:]
    else:
        joined = names[:-1] + [f"({names[-1]} z)"]
    shape = list(ap.shape)
    shape.insert(axis, n)
    return ap.rearrange(f"{' '.join(joined)} -> {' '.join(new)}", z=1).to_broadcast(shape)


def macaron_kernel(nc, x, Wq, bq, Wk, bk, Wv, bv, Wc, We, Wo, bo, gamma, beta,
                   Wr, expert_bias, Wg, Wu, Wd, Wg_s, Wu_s, Wd_s, out):
    B, S, D = x.shape
    KV = Wk.shape[1]
    L = Wc.shape[1]
    E, _, FE = Wg.shape
    FS = Wg_s.shape[1]
    FR = E * FE
    HD = 8
    G = KV // HD
    H = D // HD
    R = H // G
    QKV = D + 2 * KV
    V1 = HD + 1
    KVC = G * HD * V1
    NCH = B * S // CHUNK
    assert D == P and FR % P == 0 and FR // P + 1 == STEPS and S == 2 * P and NCH >= 5

    x_dram = x.rearrange("b s d -> (b s) d").rearrange("(c i p) d -> c p i d", i=TILES, p=P)
    out_dram = out.rearrange("b s d -> (b s) d").rearrange("(c i p) d -> c p i d", i=TILES, p=P)

    with ExitStack() as ctx:
        def sb(name, shape, dt=F32):
            return ctx.enter_context(nc.sbuf_tensor(name, shape, dt))

        def sem(name):
            return ctx.enter_context(nc.semaphore(name))

        wg_raw, wu_raw = sb("wg_raw", [P, FR + FS]), sb("wu_raw", [P, FR + FS])
        wd = sb("wd", [P, STEPS, D])
        wr_raw = sb("wr_raw", [P, E])
        wqkv_raw = sb("wqkv_raw", [P, QKV])
        wkv_in = sb("wkv_in", [P, 2 * KV])
        wo_raw = sb("wo_raw", [P, D])
        wc_in, we_in = sb("wc_in", [KV, L]), sb("we_in", [L, KV])
        bkv_col = sb("bkv_col", [KV, 2])
        bias_raw = sb("bias_raw", [1, QKV + D])
        gamma_b, beta_b, ebias_b = sb("gamma_b", [P, D]), sb("beta_b", [P, D]), sb("ebias_b", [P, E])
        wg_hi, wg_lo = sb("wg_hi", [P, FR + FS], F32R), sb("wg_lo", [P, FR + FS], F32R)
        wu_hi, wu_lo = sb("wu_hi", [P, FR + FS], F32R), sb("wu_lo", [P, FR + FS], F32R)
        wr_hi, wr_lo = sb("wr_hi", [P, E], F32R), sb("wr_lo", [P, E], F32R)
        wqkv_hi, wqkv_lo = sb("wqkv_hi", [P, QKV], F32R), sb("wqkv_lo", [P, QKV], F32R)
        wo_hi, wo_lo = sb("wo_hi", [P, D], F32R), sb("wo_lo", [P, D], F32R)
        bias_hi, bias_lo = sb("bias_hi", [1, QKV + D], F32R), sb("bias_lo", [1, QKV + D], F32R)
        wcT, wkvT, wce = sb("wcT", [L, KV]), sb("wkvT", [KV, 2, P]), sb("wce", [KV, KV])
        ident, ones, tri = sb("ident", [P, P]), sb("ones", [P, P]), sb("tri", [P, P])
        ones_row = sb("ones_row", [1, P], F32R)
        spread_raw, spread = sb("spread_raw", [2 * E, FR]), sb("spread", [2 * E, FR], F32R)
        iota_e = sb("iota_e", [P, E])
        neg_half = sb("neg_half", [P, TILES])
        x_next, x_cur = sb("x_next", [P, TILES, D]), sb("x_cur", [P, TILES, D])
        x1, x1_beta, x2, x2_cur, y_out = (
            sb(n, [P, TILES, D]) for n in ("x1", "x1_beta", "x2", "x2_cur", "y_out"))
        stats, moments, var_eps, neg_mean, rstd, normed = {}, {}, {}, {}, {}, {}
        for k in "FAZ":
            stats[k], moments[k] = sb(f"stats_{k}", [P, TILES, 6]), sb(f"moments_{k}", [P, TILES, 2])
            var_eps[k], neg_mean[k] = sb(f"var_eps_{k}", [P, TILES]), sb(f"neg_mean_{k}", [P, TILES])
            rstd[k], normed[k] = sb(f"rstd_{k}", [P, TILES]), sb(f"normed_{k}", [P, TILES, D])
        fyT_hi = [sb(f"fyT_hi{i}", [P, CHUNK], F32R) for i in range(2)]
        fyT_lo = [sb(f"fyT_lo{i}", [P, CHUNK], F32R) for i in range(2)]
        exp_neg, denom, score, biased = (sb(n, [P, TILES, E]) for n in ("exp_neg", "denom", "score", "biased"))
        top_val, top_idx = sb("top_val", [P, TILES, 8]), sb("top_idx", [P, TILES, 8], U32)
        is_first, is_second, chosen, picked = (
            sb(n, [P, TILES, E]) for n in ("is_first", "is_second", "chosen", "picked"))
        pick_sum, pick_inv = sb("pick_sum", [P, TILES]), sb("pick_inv", [P, TILES])
        pick_sum_eps = sb("pick_sum_eps", [P, TILES])
        route_w = sb("route_w", [P, TILES, E])
        route_parts = sb("route_parts", [P, TILES, 2 * E], F32R)
        wT = [sb(f"wT{i}", [2 * E, CHUNK], F32R) for i in range(2)]
        silu_g = [sb(f"silu_g{i}", [P, CHUNK]) for i in range(2)]
        gated = [sb(f"gated{i}", [P, CHUNK]) for i in range(2)]
        hidden = sb("hidden", [P, STEPS, CHUNK])
        downT = sb("downT", [P, CHUNK])
        ayT_hi, ayT_lo = sb("ayT_hi", [P, CHUNK], F32R), sb("ayT_lo", [P, CHUNK], F32R)
        qk_exp, qk_relu = sb("qk_exp", [P, TILES, D + KV]), sb("qk_relu", [P, TILES, D + KV])
        qk_feat = sb("qk_feat", [P, TILES, D + KV])
        v_ones = sb("v_ones", [P, TILES, G, V1])
        kv = sb("kv", [P, TILES, KVC])
        kv_cum = sb("kv_cum", [P, 2, KVC])
        prod = sb("prod", [P, 2, H * HD * V1])
        num_den = sb("num_den", [P, TILES, H, V1])
        den_eps, den_inv = sb("den_eps", [P, TILES, H]), sb("den_inv", [P, TILES, H])
        att_o = sb("att_o", [P, TILES, D])
        oT_hi, oT_lo = sb("oT_hi", [P, CHUNK], F32R), sb("oT_lo", [P, CHUNK], F32R)
        att_z, z_gamma = sb("att_z", [P, TILES, D]), sb("z_gamma", [P, TILES, D])
        def bank(name):
            return ctx.enter_context(nc.psum_tensor(name, [P, 512], F32))
        ps_gate, ps_up = [bank("ps_gate0"), bank("ps_gate1")], [bank("ps_up0"), bank("ps_up1")]
        ps_w, ps_down, ps_f, ps_a = bank("ps_w"), bank("ps_down"), bank("ps_f"), bank("ps_a")

        fold_loaded, ebias_loaded, att_loaded = sem("fold_loaded"), sem("ebias_loaded"), sem("att_loaded")
        wr_loaded, shared_loaded, routed_loaded, wd_loaded = (
            sem("wr_loaded"), sem("shared_loaded"), sem("routed_loaded"), sem("wd_loaded"))
        x_loaded, x_copied, x2_copied = sem("x_loaded"), sem("x_copied"), sem("x2_copied")
        zeroed, masks_made, consts_made = sem("zeroed"), sem("masks_made"), sem("consts_made")
        dve_consts = sem("dve_consts")
        fold_ready, fold_copied = sem("fold_ready"), sem("fold_copied")
        hi_made, weights_split = sem("hi_made"), sem("weights_split")
        stats_made = {k: sem(f"stats_made_{k}") for k in "FAZ"}
        moments_made = {k: sem(f"moments_made_{k}") for k in "FAZ"}
        eps_added = {k: sem(f"eps_added_{k}") for k in "FAZ"}
        rstd_made = {k: sem(f"rstd_made_{k}") for k in "FAZ"}
        norm_made = {k: sem(f"norm_made_{k}") for k in "FAZ"}
        fyT_ready, fyT_hi_made, fyT_lo_made = sem("fyT_ready"), sem("fyT_hi_made"), sem("fyT_lo_made")
        logits_ready, exp_made, w_made = sem("logits_ready"), sem("exp_made"), sem("w_made")
        sel_chain = [sem("sel_chain0"), sem("sel_chain1")]
        wT_ready, wT_copied = sem("wT_ready"), sem("wT_copied")
        gate_ready, up_ready, silu_made, hidden_made = (
            sem("gate_ready"), sem("up_ready"), sem("silu_made"), sem("hidden_made"))
        gated_made, weight_ready = sem("gated_made"), sem("weight_ready")
        down_ready, down_copied, out_ready, out_added = (
            sem("down_ready"), sem("down_copied"), sem("out_ready"), sem("out_added"))
        ayT_ready, ayT_hi_made, ayT_lo_made = sem("ayT_ready"), sem("ayT_hi_made"), sem("ayT_lo_made")
        qkv_ready, qkv_read, feat_made = sem("qkv_ready"), sem("qkv_read"), sem("feat_made")
        kv_made, cum_ready, cum_copied, red_made = (
            sem("kv_made"), sem("cum_ready"), sem("cum_copied"), sem("red_made"))
        prod_made = [sem("prod_made0"), sem("prod_made1")]
        den_chain, o_made = sem("den_chain"), sem("o_made")
        oT_ready, oT_hi_made, oT_lo_made = sem("oT_ready"), sem("oT_hi_made"), sem("oT_lo_made")
        z_ready, z_added, z_scaled, x2_made, beta_added = (
            sem("z_ready"), sem("z_added"), sem("z_scaled"), sem("x2_made"), sem("beta_added"))
        out_stored = sem("out_stored")

        waits_passed = sem("waits_passed")

        SEL_CHAIN = 2 * STEPS

        def slot1(c):
            return c if isinstance(c, int) and c < 2 else 2 * c - 2

        def slot2(c):
            return c + NCH if isinstance(c, int) and c >= NCH - 2 else 2 * c + 3

        def need(eng, semaphore, value):
            if not isinstance(value, int) or value > 0:
                eng.wait_ge(semaphore, value)

        def need_apart(eng, semaphore, value):
            if not isinstance(value, int) or value > 0:
                eng.wait_ge(semaphore, value).then_inc(waits_passed, 1)

        def vector_multiplies(c):
            return isinstance(c, int) and c in (0, 1, NCH - 1)

        def multiply_features(eng, c, i):
            need(eng, cum_copied, TILES * c + i + 1)
            need(eng, red_made, TILES * c + i - 1)
            for g in range(G):
                qf = qk_feat[:, i, g * R * HD:(g + 1) * R * HD].rearrange("p (r f) -> p r f", r=R)
                cum = kv_cum[:, i % 2, g * HD * V1:(g + 1) * HD * V1].rearrange("p (f v) -> p f v", f=HD)
                dst = prod[:, i % 2, g * R * HD * V1:(g + 1) * R * HD * V1]
                last = eng.tensor_tensor(dst.rearrange("p (r f v) -> p r f v", r=R, f=HD),
                                         broadcast_free(qf, 3, V1), broadcast_free(cum, 1, R), ALU.mult)
            last.then_inc(prod_made[i % 2], 1)

        def walk(eng, do):
            def entry(name, args):
                name, *number = name.split(":")
                if name in do:
                    do[name](*args, *map(int, number))

            def ffn_args(which, c):
                slot = slot1(c) if which == 1 else slot2(c)
                return slot, slot % 2 if isinstance(slot, int) else which - 1, which, c

            def run(ffn, table, args):
                for m in range(len(table)):
                    for name in table[m]:
                        kind = name.split("_")[0]
                        if kind == "ffn" and ffn is not None:
                            entry(name, (ffn[0], ffn[1], m, (ffn[1] + m) % 2))
                        elif kind == "now" and ffn is not None:
                            entry(name.replace("now", "in"), ffn)
                        elif kind == "prev" and kind in args:
                            entry(name.replace("prev", "att"), args[kind])
                        elif kind in args:
                            entry(name, args[kind])

            def slot_y(n):
                run(ffn_args(2, n - 2), Y_TABLE, {"out": ffn_args(1, n), "att": (n,), "end": (n - 1,), "x": (n + 1,),
                                                  "in": ffn_args(1, n + 1)})

            def slot_x(n):
                run(ffn_args(1, n), X_TABLE, {"out": ffn_args(2, n - 3), "att": (n - 1,), "x2": (n - 2,),
                                              "in": ffn_args(2, n - 2)})

            entry("x_copy", (0,))
            run(None, START_TABLE, {"start": (), "in": ffn_args(1, 0)})
            run(ffn_args(1, 0), Y_TABLE, {"in": ffn_args(1, 1)})
            run(ffn_args(1, 1), FIRST_TABLE, {"out": ffn_args(1, 0), "att": (0,), "x": (1,), "in": ffn_args(1, 2)})
            run(ffn_args(1, 2), RAMP_TABLE, {"prev": (0,), "out": ffn_args(1, 1), "end": (0,), "att": (1,), "x": (2,),
                                             "x2": (0,), "in": ffn_args(2, 0)})
            slot_y(2)
            slot_x(3)
            with eng.Fori(3, NCH - 1) as n:
                slot_y(n)
                slot_x(n + 1)
            last = NCH - 1
            run(ffn_args(2, last - 2), TAIL_TABLE,
                {"out": ffn_args(1, last), "end": (last - 1,), "att": (last,), "in": ffn_args(2, last - 1)})
            run(ffn_args(2, last - 1), LATE_TABLE,
                {"out": ffn_args(2, last - 2), "att": (last,), "x2": (last - 1,), "end": (last,),
                 "in": ffn_args(2, last)})
            run(ffn_args(2, last), X_TABLE, {"out": ffn_args(2, last - 1), "x2": (last,)})
            run(None, X_TABLE, {"out": ffn_args(2, last)})

        block = ctx.enter_context(nc.Block())

        @block.sync
        def _(sp):
            sp.dma_start(x_next[:], x_dram[0]).then_inc(x_loaded, 16)
            for dst, src in ((wc_in[:], Wc), (wkv_in[:, 0:KV], Wk), (wkv_in[:, KV:2 * KV], Wv), (we_in[:], We),
                             (bkv_col[:, 0:1], bk.rearrange("(p a) -> p a", a=1)),
                             (bkv_col[:, 1:2], bv.rearrange("(p a) -> p a", a=1))):
                sp.dma_start(dst, src).then_inc(fold_loaded, 16)
            sp.dma_start(ebias_b[:], expert_bias.rearrange("(a d) -> a d", a=1).to_broadcast([P, E])
                         ).then_inc(ebias_loaded, 16)
            sp.dma_start(wd[0:FS, 0, :], Wd_s).then_inc(wd_loaded, 16)
            sp.dma_start(wd[:, 1:STEPS, :],
                         Wd.rearrange("e f d -> (e f) d").rearrange("(m p) d -> p m d", p=P)).then_inc(wd_loaded, 16)
            for dst, src in ((wqkv_raw[:, 0:D], Wq), (wo_raw[:], Wo),
                             (bias_raw[:, 0:D], bq.rearrange("(a d) -> a d", a=1)),
                             (bias_raw[:, QKV:QKV + D], bo.rearrange("(a d) -> a d", a=1)),
                             (gamma_b[:], gamma.rearrange("(a d) -> a d", a=1).to_broadcast([P, D])),
                             (beta_b[:], beta.rearrange("(a d) -> a d", a=1).to_broadcast([P, D]))):
                sp.dma_start(dst, src).then_inc(att_loaded, 16)

            def x_load(c):
                need_apart(sp, x_copied, c)
                need_apart(sp, norm_made["F"], slot1(c - 1) + 1)
                sp.dma_start(x_next[:], x_dram[c]).then_inc(x_loaded, 16)

            x_load(1)
            x_load(2)
            with sp.Fori(3, NCH) as c:
                x_load(c)
            sp.wait_ge(out_stored, 16 * NCH)

        @block.gpsimd
        def _(pool):
            pool.memset(ident[:], 0.0)
            pool.memset(ones[:], 1.0)
            pool.memset(spread_raw[:], 0.0)
            pool.memset(neg_half[:], -0.5).then_inc(zeroed, 1)
            pool.wait_ge(zeroed, 1)
            pool.affine_select(out=ident[:], in_=ident[:], compare_op=ALU.not_equal, fill=1.0, base=0,
                               pattern=[[-1, P]], channel_multiplier=1)
            pool.affine_select(out=tri[:], in_=ones[:], compare_op=ALU.is_ge, fill=0.0, base=0,
                               pattern=[[1, P]], channel_multiplier=-1)
            pool.affine_select(out=spread_raw[:], in_=spread_raw[:], compare_op=ALU.not_equal, fill=1.0, base=0,
                               pattern=[[-1, E], [0, FE]], channel_multiplier=1).then_inc(zeroed, 1)
            pool.wait_ge(zeroed, 2)
            pool.affine_select(out=spread_raw[:], in_=spread_raw[:], compare_op=ALU.not_equal, fill=1.0, base=-E,
                               pattern=[[-1, E], [0, FE]], channel_multiplier=1).then_inc(masks_made, 1)

            def normalise(k, slot, source, free):
                need_apart(pool, moments_made[k], slot + 1)
                pool.tensor_scalar(var_eps[k][:], moments[k][:, :, 1], 1.0, LN_EPS, ALU.mult, ALU.add)
                pool.tensor_scalar(neg_mean[k][:], moments[k][:, :, 0], -1.0, 0.0, ALU.mult, ALU.add
                                   ).then_inc(eps_added[k], 1)
                need(pool, eps_added[k], slot + 1)
                pool.tensor_tensor(rstd[k][:], var_eps[k][:], neg_half[:], ALU.pow).then_inc(rstd_made[k], 1)
                free()
                need_apart(pool, rstd_made[k], slot + 1)
                for i in range(TILES):
                    last = pool.tensor_scalar(normed[k][:, i, :], source[:, i, :], neg_mean[k][:, i:i + 1],
                                              rstd[k][:, i:i + 1], ALU.add, ALU.mult)
                last.then_inc(norm_made[k], 1)

            def in_norm(slot, copy, which, c):
                def free():
                    need(pool, fyT_ready, slot)
                normalise("F", slot, x_next if which == 1 else x2, free)

            def att_norm(c):
                def free():
                    need(pool, z_added, c)
                normalise("A", c, x1, free)

            def att_beta(c):
                need(pool, x2_made, c)
                need(pool, out_added, slot1(c) + 1)
                pool.tensor_tensor(x1_beta[:], x1[:], broadcast_free(beta_b[:], 1, TILES), ALU.add
                                   ).then_inc(beta_added, 1)

            def end_norm(c):
                def free():
                    need(pool, z_scaled, c)
                normalise("Z", c, att_z, free)

            def att_kv(c, i):
                need(pool, feat_made, 2 * c + i // 2 + 1)
                if i == 0:
                    need(pool, cum_ready, TILES * c)
                key = qk_feat[:, i, D:D + KV].rearrange("p (g f) -> p g f", g=G)
                pool.tensor_tensor(kv[:, i, :].rearrange("p (g f v) -> p g f v", g=G, f=HD),
                                   broadcast_free(key, 3, V1), broadcast_free(v_ones[:, i], 2, HD), ALU.mult
                                   ).then_inc(kv_made, 1)

            def att_mul(c, i):
                if not (i % 2 and vector_multiplies(c)):
                    multiply_features(pool, c, i)

            def start_att():
                pool.wait_ge(att_loaded, 16 * 6)

            walk(pool, {"start_att": start_att, "in_norm": in_norm, "att_norm": att_norm, "end_norm": end_norm,
                        "att_beta": att_beta, "att_kv": att_kv, "att_mul": att_mul})

        @block.scalar
        def _(act):
            act.dma_start(wr_raw[:], Wr).then_inc(wr_loaded, 16)
            act.dma_start(wg_raw[:, 0:FS], Wg_s).then_inc(shared_loaded, 16)
            act.dma_start(wu_raw[:, 0:FS], Wu_s).then_inc(shared_loaded, 16)
            act.dma_start(wg_raw[:, FS:FS + FR].rearrange("p (e f) -> p e f", e=E), Wg.rearrange("e d f -> d e f")
                          ).then_inc(routed_loaded, 16)
            act.dma_start(wu_raw[:, FS:FS + FR].rearrange("p (e f) -> p e f", e=E), Wu.rearrange("e d f -> d e f")
                          ).then_inc(routed_loaded, 16)

            def start_route():
                act.wait_ge(wr_loaded, 16)
                act.copy(wr_hi[:], wr_raw[:]).then_inc(hi_made, 1)

            def start_ffn(k):
                act.wait_ge((shared_loaded, routed_loaded)[k], 32)
                f = (slice(0, FS), slice(FS, FS + FR))[k]
                act.copy(wg_hi[:, f], wg_raw[:, f]).then_inc(hi_made, 1)
                act.copy(wu_hi[:, f], wu_raw[:, f]).then_inc(hi_made, 1)

            def start_att():
                act.wait_ge(att_loaded, 16 * 6)
                act.wait_ge(fold_copied, 4)
                act.copy(wqkv_hi[:], wqkv_raw[:]).then_inc(hi_made, 1)
                act.copy(wo_hi[:], wo_raw[:]).then_inc(hi_made, 1)
                act.copy(bias_hi[:], bias_raw[:]).then_inc(hi_made, 1)

            def x_copy(c):
                need(act, x_loaded, 16 * (c + 1))
                need(act, out_added, slot1(c - 1) + 1 if not (isinstance(c, int) and c == 0) else 0)
                act.copy(x_cur[:], x_next[:]).then_inc(x_copied, 1)

            def out_store(slot, copy, which, c):
                if which == 2:
                    need(act, out_added, slot + 1)
                    act.dma_start(out_dram[c], y_out[:]).then_inc(out_stored, 16)

            def x2_copy(c):
                need(act, x2_made, c + 1)
                if not (isinstance(c, int) and c == 0):
                    need(act, out_added, slot2(c - 1) + 1)
                act.copy(x2_cur[:], x2[:]).then_inc(x2_copied, 1)

            def in_hi(slot, copy, which, c):
                need(act, fyT_ready, slot + 1)
                act.copy(fyT_hi[copy][:], ps_f[:]).then_inc(fyT_hi_made, 1)

            def in_exp(slot, copy, which, c):
                need(act, logits_ready, slot + 1)
                need(act, w_made, slot)
                act.activation(exp_neg[:], ps_f[:, 0:TILES * E].rearrange("p (i e) -> p i e", e=E), ACT.Exp,
                               scale=-1.0).then_inc(exp_made, 1)

            def in_wT_copy(slot, copy, which, c):
                need(act, wT_ready, slot + 1)
                act.copy(wT[copy][:], ps_f[0:2 * E, :]).then_inc(wT_copied, 1)

            def ffn_up(slot, copy, m, b):
                rows = P if m > 0 else FS
                need(act, gate_ready, STEPS * slot + m + 1)
                need(act, hidden_made, STEPS * slot + m - 1)
                act.activation(silu_g[b][0:rows, :], ps_gate[b][0:rows, :], ACT.Silu).then_inc(silu_made, 1)

            def out_copy(slot, copy, which, c):
                need(act, down_ready, slot + 1)
                need(act, out_ready, slot)
                act.copy(downT[:], ps_down[:]).then_inc(down_copied, 1)

            def att_hi(c):
                need(act, ayT_ready, c + 1)
                act.copy(ayT_hi[:], ps_a[:]).then_inc(ayT_hi_made, 1)

            def att_exp(c, j):
                t = slice(2 * j, 2 * j + 2)
                need(act, qkv_ready, 2 * c + j + 1)
                if j == 0:
                    need(act, feat_made, 2 * c)
                    need(act, kv_made, TILES * c)
                src = (ps_a, ps_f)[j][:, 0:2 * QKV].rearrange("p (i q) -> p i q", i=2)
                act.activation(qk_exp[:, t, :], src[:, :, 0:D + KV], ACT.Exp)
                act.activation(qk_relu[:, t, :], src[:, :, 0:D + KV], ACT.Relu)
                for i in range(2):
                    last = act.copy(v_ones[:, 2 * j + i, :, 0:HD],
                                    src[:, i, D + KV:QKV].rearrange("p (g v) -> p g v", g=G))
                last.then_inc(qkv_read, 1)

            def att_cum_copy(c, i):
                need(act, cum_ready, TILES * c + i + 1)
                need(act, prod_made[i % 2], 2 * c + i // 2)
                act.copy(kv_cum[:, i % 2, :], ps_a[:, 0:KVC]).then_inc(cum_copied, 1)

            def end_o_hi(c):
                need(act, oT_ready, c + 1)
                act.copy(oT_hi[:], ps_a[:]).then_inc(oT_hi_made, 1)

            walk(act, {"start_route": start_route, "start_ffn": start_ffn, "start_att": start_att, "x_copy": x_copy,
                       "x2_copy": x2_copy, "out_store": out_store, "in_hi": in_hi, "in_exp": in_exp,
                       "in_wT_copy": in_wT_copy, "ffn_up": ffn_up, "out_copy": out_copy, "att_hi": att_hi,
                       "att_exp": att_exp, "att_cum_copy": att_cum_copy, "end_o_hi": end_o_hi})

        @block.vector
        def _(dve):
            dve.memset(v_ones[:], 1.0).then_inc(dve_consts, 1)
            for e in range(E):
                last = dve.memset(iota_e[:, e:e + 1], float(e))
            last.then_inc(dve_consts, 1)

            def start_consts():
                dve.wait_ge(masks_made, 1)
                dve.tensor_copy(spread[:], spread_raw[:])
                dve.tensor_copy(ones_row[:], ones[0:1, :]).then_inc(consts_made, 1)

            def start_fold(k):
                dve.wait_ge(fold_ready, k + 1)
                if k == 0:
                    dve.tensor_copy(wcT[:], ps_a[0:L, 0:KV])
                    dve.tensor_copy(wkvT[:], ps_a[0:KV, P:3 * P].rearrange("p (a b) -> p a b", a=2)
                                    ).then_inc(fold_copied, 1)
                if k == 1:
                    dve.tensor_copy(wce[:], ps_a[0:KV, 0:KV]).then_inc(fold_copied, 1)
                if k == 2:
                    dve.tensor_copy(wqkv_raw[:, D:QKV], ps_a[:, 0:2 * KV]).then_inc(fold_copied, 1)
                    dve.tensor_copy(bias_raw[:, D:QKV], ps_a[0:1, 2 * KV:4 * KV]).then_inc(fold_copied, 1)

            def low_part(n, lo, hi, raw):
                dve.wait_ge(hi_made, n)
                dve.tensor_tensor(lo, raw, hi.bitcast(F32), ALU.subtract).then_inc(weights_split, 1)

            def start_route():
                low_part(1, wr_lo[:], wr_hi[:], wr_raw[:])
                dve.wait_ge(ebias_loaded, 16)

            def start_ffn(k):
                f = (slice(0, FS), slice(FS, FS + FR))[k]
                low_part(2 + 2 * k, wg_lo[:, f], wg_hi[:, f], wg_raw[:, f])
                low_part(3 + 2 * k, wu_lo[:, f], wu_hi[:, f], wu_raw[:, f])

            def start_att():
                dve.wait_ge(att_loaded, 16 * 6)
                for n, (lo, hi, raw) in enumerate(((wqkv_lo, wqkv_hi, wqkv_raw), (wo_lo, wo_hi, wo_raw),
                                                   (bias_lo, bias_hi, bias_raw))):
                    low_part(6 + n, lo[:], hi[:], raw[:])

            def statistics(k, slot, source):
                for i in range(TILES):
                    last = dve.bn_stats(stats[k][:, i, :], source[:, i, :])
                last.then_inc(stats_made[k], 1)

            def aggregate(k, slot):
                need(dve, stats_made[k], slot + 1)
                need_apart(dve, norm_made[k], slot)
                for i in range(TILES):
                    last = dve.bn_aggr(moments[k][:, i, :], stats[k][:, i, :])
                last.then_inc(moments_made[k], 1)

            def in_stat(slot, copy, which, c):
                if which == 1:
                    need(dve, x_loaded, 16 * (c + 1))
                    statistics("F", slot, x_next)
                else:
                    need(dve, x2_made, c + 1)
                    statistics("F", slot, x2)

            def in_aggr(slot, copy, which, c):
                aggregate("F", slot)

            def in_lo(slot, copy, which, c):
                need(dve, fyT_hi_made, slot + 1)
                dve.tensor_tensor(fyT_lo[copy][:], ps_f[:], fyT_hi[copy][:].bitcast(F32), ALU.subtract
                                  ).then_inc(fyT_lo_made, 1)

            def in_sel(slot, copy, which, c, k):
                wait = need_apart if k in (3, 4) else need
                if k > 0:
                    before = k - 1 - (k == 6)
                    wait(dve, sel_chain[before // STEPS], STEPS * slot + before % STEPS + 1)
                if k == 0:
                    need(dve, exp_made, slot + 1)
                    need(dve, wT_ready, slot)
                    ins = dve.tensor_scalar(denom[:], exp_neg[:], 1.0, None, ALU.add)
                if k == 1:
                    ins = dve.reciprocal(score[:], denom[:])
                if k == 2:
                    ins = dve.tensor_tensor(biased[:], score[:], broadcast_free(ebias_b[:], 1, TILES), ALU.add)
                if k == 3:
                    for i in range(TILES):
                        ins = dve.max(top_val[:, i, :], biased[:, i, :])
                if k == 4:
                    for i in range(TILES):
                        ins = dve.max_index(top_idx[:, i, :], top_val[:, i, :], biased[:, i, :])
                if k in (5, 6):
                    ins = dve.tensor_tensor((is_first, is_second)[k - 5][:], broadcast_free(iota_e[:], 1, TILES),
                                            top_idx[:, :, k - 5:k - 4].to_broadcast([P, TILES, E]), ALU.is_equal)
                if k == 7:
                    ins = dve.tensor_tensor(chosen[:], is_first[:], is_second[:], ALU.add)
                if k == 8:
                    ins = dve.tensor_tensor(picked[:], score[:], chosen[:], ALU.mult)
                if k == 9:
                    ins = dve.tensor_reduce(pick_sum[:], picked[:], AX_X, ALU.add)
                if k == 10:
                    ins = dve.tensor_scalar(pick_sum_eps[:], pick_sum[:], ROUTE_EPS, None, ALU.add)
                if k == 11:
                    ins = dve.reciprocal(pick_inv[:], pick_sum_eps[:])
                if k == 12:
                    ins = dve.tensor_tensor(route_w[:], picked[:], broadcast_free(pick_inv[:], 2, E), ALU.mult)
                if k == 13:
                    ins = dve.tensor_copy(route_parts[:, :, 0:E], route_w[:])
                if k == SEL_CHAIN:
                    dve.tensor_tensor(route_parts[:, :, E:2 * E], route_w[:], route_parts[:, :, 0:E].bitcast(F32),
                                      ALU.subtract).then_inc(w_made, 1)
                else:
                    ins.then_inc(sel_chain[k // STEPS], 1)

            def ffn_gated(slot, copy, m, b):
                routed = m > 0
                rows = P if routed else FS
                need(dve, silu_made, STEPS * slot + m + 1)
                need(dve, up_ready, STEPS * slot + m + 1)
                if routed:
                    dve.tensor_tensor(gated[b][:], silu_g[b][:], ps_up[b][:], ALU.mult
                                      ).then_inc(gated_made, 2 if m == 1 else 1)
                else:
                    dve.tensor_tensor(hidden[0:rows, m, :], silu_g[b][0:rows, :], ps_up[b][0:rows, :], ALU.mult
                                      ).then_inc(hidden_made, 1)

            def ffn_hidden(slot, copy, m, b):
                if m > 0:
                    need(dve, gated_made, STEPS * slot + m + 1)
                    need(dve, weight_ready, STEPS * slot + m + 1)
                    dve.tensor_tensor(hidden[:, m, :], gated[b][:], ps_w[:], ALU.mult).then_inc(hidden_made, 1)

            def out_add(slot, copy, which, c):
                need(dve, out_ready, slot + 1)
                if which == 1:
                    need(dve, x_copied, c + 1)
                    need(dve, beta_added, c)
                    src, dst = x_cur, x1
                else:
                    need(dve, x2_copied, c + 1)
                    need(dve, out_stored, 16 * c)
                    src, dst = x2_cur, y_out
                dve.scalar_tensor_tensor(out=dst[:], in0=ps_f[:].rearrange("p (i d) -> p i d", i=TILES), scalar=0.5,
                                         in1=src[:], op0=ALU.mult, op1=ALU.add).then_inc(out_added, 1)

            def att_stat(c):
                need(dve, out_added, slot1(c) + 1)
                statistics("A", c, x1)

            def att_aggr(c):
                aggregate("A", c)

            def att_lo(c):
                need(dve, ayT_hi_made, c + 1)
                dve.tensor_tensor(ayT_lo[:], ps_a[:], ayT_hi[:].bitcast(F32), ALU.subtract).then_inc(ayT_lo_made, 1)

            def att_feat(c, j):
                t = slice(2 * j, 2 * j + 2)
                need(dve, qkv_read, 2 * c + j + 1)
                if j == 0:
                    need(dve, prod_made[0], 2 * c)
                    need(dve, prod_made[1], 2 * c)
                dve.scalar_tensor_tensor(out=qk_feat[:, t, :], in0=qk_exp[:, t, :], scalar=1.0,
                                         in1=qk_relu[:, t, :], op0=ALU.min, op1=ALU.add).then_inc(feat_made, 1)

            def att_red(c, i):
                if i % 2 and vector_multiplies(c):
                    multiply_features(dve, c, i)
                need(dve, prod_made[i % 2], 2 * c + i // 2 + 1)
                dve.tensor_reduce(num_den[:, i], prod[:, i % 2, :].rearrange("p (h f v) -> p h v f", h=H, f=HD),
                                  AX_X, ALU.add).then_inc(red_made, 1)

            def end_div(c, k):
                if k == 0:
                    need(dve, red_made, TILES * (c + 1))
                    dve.tensor_scalar(den_eps[:], num_den[:, :, :, HD], DEN_EPS, None, ALU.add).then_inc(den_chain, 1)
                if k == 1:
                    need(dve, den_chain, 2 * c + 1)
                    dve.reciprocal(den_inv[:], den_eps[:]).then_inc(den_chain, 1)
                if k == 2:
                    need(dve, den_chain, 2 * c + 2)
                    need(dve, oT_ready, c)
                    dve.tensor_tensor(att_o[:].rearrange("p i (h v) -> p i h v", h=H), num_den[:, :, :, 0:HD],
                                      broadcast_free(den_inv[:], 3, HD), ALU.mult).then_inc(o_made, 1)

            def end_o_lo(c):
                need(dve, oT_hi_made, c + 1)
                dve.tensor_tensor(oT_lo[:], ps_a[:], oT_hi[:].bitcast(F32), ALU.subtract).then_inc(oT_lo_made, 1)

            def end_res(c):
                need(dve, z_ready, c + 1)
                need(dve, norm_made["Z"], c)
                dve.tensor_tensor(att_z[:], ps_a[:].rearrange("p (i d) -> p i d", i=TILES), normed["A"][:], ALU.add
                                  ).then_inc(z_added, 1)

            def end_stat(c):
                need(dve, z_added, c + 1)
                statistics("Z", c, att_z)

            def end_aggr(c):
                aggregate("Z", c)

            def end_zg(c):
                need(dve, norm_made["Z"], c + 1)
                dve.tensor_tensor(z_gamma[:], normed["Z"][:], broadcast_free(gamma_b[:], 1, TILES), ALU.mult
                                  ).then_inc(z_scaled, 1)

            def end_x2(c):
                need(dve, z_scaled, c + 1)
                need(dve, beta_added, c + 1)
                need(dve, x2_copied, c)
                if not (isinstance(c, int) and c == 0):
                    need(dve, norm_made["F"], slot2(c - 1) + 1)
                dve.tensor_tensor(x2[:], z_gamma[:], x1_beta[:], ALU.add).then_inc(x2_made, 1)

            walk(dve, {"start_consts": start_consts, "start_fold": start_fold, "start_route": start_route,
                       "start_ffn": start_ffn, "start_att": start_att, "in_stat": in_stat, "in_aggr": in_aggr,
                       "att_aggr": att_aggr, "end_stat": end_stat, "end_aggr": end_aggr, "end_zg": end_zg,
                       "in_lo": in_lo, "in_sel": in_sel, "ffn_gated": ffn_gated, "ffn_hidden": ffn_hidden,
                       "out_add": out_add, "att_stat": att_stat, "att_lo": att_lo, "att_feat": att_feat,
                       "att_red": att_red, "end_div": end_div, "end_o_lo": end_o_lo, "end_res": end_res,
                       "end_x2": end_x2})

        @block.tensor
        def _(pe):
            def start_fold(k):
                if k == 0:
                    pe.wait_ge(masks_made, 1)
                    pe.wait_ge(fold_loaded, 16 * 6)
                    pe.transpose(ps_a[0:L, 0:KV], wc_in[:], ident[0:KV, 0:KV])
                    for j in range(2):
                        last = pe.transpose(ps_a[0:KV, (1 + j) * P:(2 + j) * P], wkv_in[:, j * KV:(j + 1) * KV],
                                            ident[:])
                if k == 1:
                    pe.wait_ge(fold_copied, 1)
                    last = pe.matmul(ps_a[0:KV, 0:KV], wcT[:], we_in[:], start=True, stop=True)
                if k == 2:
                    pe.wait_ge(fold_copied, 2)
                    for j in range(2):
                        pe.matmul(ps_a[:, j * KV:(j + 1) * KV], wkvT[:, j, :], wce[:], start=True, stop=True)
                    for j in range(2):
                        last = pe.matmul(ps_a[0:1, (2 + j) * KV:(3 + j) * KV], bkv_col[:, j:j + 1], wce[:],
                                         start=True, stop=True)
                last.then_inc(fold_ready, 1)

            def first_use(slot, m, semaphore, value):
                if isinstance(slot, int) and slot == 0 and m < 2:
                    pe.wait_ge(semaphore, value)

            def in_yT(slot, copy, which, c):
                need(pe, norm_made["F"], slot + 1)
                need(pe, out_added, slot - 1)
                if isinstance(slot, int) and slot in (2, 3):
                    need(pe, qkv_read, 2 * (slot - 1))
                if isinstance(slot, int) and slot == 2 * NCH - 2:
                    need(pe, qkv_read, 2 * NCH)
                if isinstance(slot, int) and slot == 0:
                    pe.wait_ge(masks_made, 1)
                for i in range(TILES):
                    last = pe.transpose(ps_f[:, i * P:(i + 1) * P], normed["F"][:, i, :], ident[:])
                last.then_inc(fyT_ready, 1)

            def in_route(slot, copy, which, c):
                need(pe, fyT_lo_made, slot + 1)
                first_use(slot, 0, weights_split, 1)
                for i in range(TILES):
                    dst, t = ps_f[:, i * E:(i + 1) * E], slice(i * P, (i + 1) * P)
                    pe.matmul(dst, fyT_hi[copy][:, t], wr_hi[:], start=True, stop=False)
                    pe.matmul(dst, fyT_hi[copy][:, t], wr_lo[:], start=False, stop=False)
                    last = pe.matmul(dst, fyT_lo[copy][:, t], wr_hi[:], start=False, stop=True)
                last.then_inc(logits_ready, 1)

            def in_wT(slot, copy, which, c):
                need(pe, w_made, slot + 1)
                if which == 1 and not (isinstance(c, int) and c <= 2):
                    need(pe, qkv_read, 2 * c)
                for i in range(TILES):
                    last = pe.transpose(ps_f[0:2 * E, i * P:(i + 1) * P], route_parts[:, i, :].bitcast(F32), ident[:])
                last.then_inc(wT_ready, 1)

            def down(slot, m):
                rows = P if m > 0 else FS
                need(pe, hidden_made, STEPS * slot + m + 1)
                if m == 0:
                    need(pe, down_copied, slot)
                    first_use(slot, m, wd_loaded, 16 * 2)
                last = pe.matmul(ps_down[:], wd[0:rows, m, :], hidden[0:rows, m, :], start=(m == 0),
                                 stop=(m == STEPS - 1))
                if m == STEPS - 1:
                    last.then_inc(down_ready, 1)

            def split_matmul(dst, w_hi, w_lo, y_hi, y_lo):
                pe.matmul(dst, w_hi, y_hi, start=True, stop=False)
                pe.matmul(dst, w_hi, y_lo, start=False, stop=False)
                return pe.matmul(dst, w_lo, y_hi, start=False, stop=True)

            def ffn_up(slot, copy, m, b):
                rows = P if m > 0 else FS
                f = slice(0, FS) if m == 0 else slice(FS + (m - 1) * P, FS + m * P)
                t = STEPS * slot + m
                if m == 0:
                    need(pe, fyT_lo_made, slot + 1)
                first_use(slot, m, weights_split, 3 + 2 * m)
                need(pe, silu_made, t - 1)
                split_matmul(ps_gate[b][0:rows, :], wg_hi[:, f], wg_lo[:, f], fyT_hi[copy][:], fyT_lo[copy][:]
                             ).then_inc(gate_ready, 1)
                if m == 2:
                    need(pe, hidden_made, t - 1)
                else:
                    need(pe, gated_made, t - 1)
                split_matmul(ps_up[b][0:rows, :], wu_hi[:, f], wu_lo[:, f], fyT_hi[copy][:], fyT_lo[copy][:]
                             ).then_inc(up_ready, 1)

            def ffn_down(slot, copy, m, b):
                down(slot, m - 2)

            def ffn_w(slot, copy, m, b):
                if m == 1:
                    need(pe, wT_copied, slot + 1)
                    first_use(slot, m, consts_made, 1)
                need(pe, hidden_made, STEPS * slot + m)
                pe.matmul(ps_w[:], spread[:, (m - 1) * P:m * P], wT[copy][:], start=True, stop=True
                          ).then_inc(weight_ready, 2 if m == 1 else 1)

            def out_down(slot, copy, which, c):
                down(slot, STEPS - 2)
                down(slot, STEPS - 1)

            def out_T(slot, copy, which, c):
                need(pe, down_copied, slot + 1)
                need(pe, wT_copied, slot + 1 if isinstance(slot, int) and slot == 2 * NCH - 1 else slot + 2)
                for i in range(TILES):
                    last = pe.transpose(ps_f[:, i * P:(i + 1) * P], downT[:, i * P:(i + 1) * P], ident[:])
                last.then_inc(out_ready, 1)

            def att_yT(c):
                need(pe, norm_made["A"], c + 1)
                need(pe, z_added, c)
                for i in range(TILES):
                    last = pe.transpose(ps_a[:, i * P:(i + 1) * P], normed["A"][:, i, :], ident[:])
                last.then_inc(ayT_ready, 1)

            def bias_and_split(dst, y_hi, y_lo, w_hi, w_lo, cols):
                pe.matmul(dst, ones_row[:], bias_hi[:, cols], start=True, stop=False)
                pe.matmul(dst, ones_row[:], bias_lo[:, cols], start=False, stop=False)
                pe.matmul(dst, y_hi, w_hi[:], start=False, stop=False)
                pe.matmul(dst, y_hi, w_lo[:], start=False, stop=False)
                return pe.matmul(dst, y_lo, w_hi[:], start=False, stop=True)

            def att_qkv(c, j):
                if j == 0:
                    need(pe, ayT_lo_made, c + 1)
                    if isinstance(c, int) and c == 0:
                        pe.wait_ge(weights_split, 8)
                elif isinstance(c, int) and c in (0, 1, NCH - 1):
                    need(pe, out_added, slot1(c) + 1)
                else:
                    need(pe, exp_made, slot1(c + 1) + 1)
                for i in range(2):
                    t = slice((2 * j + i) * P, (2 * j + i + 1) * P)
                    last = bias_and_split((ps_a, ps_f)[j][:, i * QKV:(i + 1) * QKV], ayT_hi[:, t], ayT_lo[:, t],
                                          wqkv_hi, wqkv_lo, slice(0, QKV))
                last.then_inc(qkv_ready, 1)

            def att_cum(c, i):
                need(pe, kv_made, TILES * c + i + 1)
                if i == 0:
                    need(pe, qkv_read, 2 * c + 2)
                else:
                    need(pe, cum_copied, TILES * c + i)
                if i % 2:
                    pe.matmul(ps_a[:, 0:KVC], ones[:], kv[:, i - 1, :], start=True, stop=False)
                pe.matmul(ps_a[:, 0:KVC], tri[:], kv[:, i, :], start=(i % 2 == 0), stop=True).then_inc(cum_ready, 1)

            def end_oT(c):
                need(pe, o_made, c + 1)
                need(pe, cum_copied, TILES * (c + 1))
                for i in range(TILES):
                    last = pe.transpose(ps_a[:, i * P:(i + 1) * P], att_o[:, i, :], ident[:])
                last.then_inc(oT_ready, 1)

            def end_proj(c):
                need(pe, oT_lo_made, c + 1)
                for i in range(TILES):
                    t = slice(i * P, (i + 1) * P)
                    last = bias_and_split(ps_a[:, t], oT_hi[:, t], oT_lo[:, t], wo_hi, wo_lo, slice(QKV, QKV + D))
                last.then_inc(z_ready, 1)

            walk(pe, {"start_fold": start_fold, "in_yT": in_yT, "in_route": in_route, "in_wT": in_wT,
                      "ffn_up": ffn_up, "ffn_down": ffn_down, "ffn_w": ffn_w, "out_down": out_down, "out_T": out_T,
                      "att_yT": att_yT, "att_qkv": att_qkv, "att_cum": att_cum, "end_oT": end_oT,
                      "end_proj": end_proj})


_INS = ["L0_attn_x", "L0_attn_Wq", "L0_attn_bq", "L0_attn_Wk", "L0_attn_bk", "L0_attn_Wv", "L0_attn_bv",
        "L0_attn_Wc", "L0_attn_We", "L0_attn_Wo", "L0_attn_bo", "L0_attn_gamma", "L0_attn_beta",
        "L0_ffn_W_gate_router", "L0_ffn_expert_bias", "L0_ffn_Wg", "L0_ffn_Wu", "L0_ffn_Wd",
        "L0_ffn_Wg_s", "L0_ffn_Wu_s", "L0_ffn_Wd_s"]


def kernel(**inputs):
    import numpy as _np
    import concourse.bacc as _bacc
    from concourse import mybir as _mybir
    from concourse.bass_utils import run_bass_kernel_spmd as _run

    nc = _bacc.Bacc("TRN2", target_bir_lowering=False, num_devices=1)
    arrays, args = {}, []
    for name in _INS:
        a = _np.ascontiguousarray(inputs[name])
        arrays[f"in_{name}"] = a
        args.append(nc.dram_tensor(f"in_{name}", a.shape, _mybir.dt.from_np(a.dtype), kind="ExternalInput").ap())
    shape = inputs["L0_attn_x"].shape
    args.append(nc.dram_tensor("out_0", shape, _mybir.dt.float32, kind="ExternalOutput").ap())
    macaron_kernel(nc, *args)
    r = _run(nc, [arrays], core_ids=[0])
    return r.results[0]["out_0"]
```

```python
from contextlib import ExitStack

import concourse.bass as bass
from concourse import mybir

ALU = mybir.AluOpType
ACT = mybir.ActivationFunctionType
F32 = mybir.dt.float32
F32R = mybir.dt.float32r
U32 = mybir.dt.uint32
AX_X = mybir.AxisListType.X

P = 128
LN_EPS = 1e-5
DEN_EPS = 1e-6
ROUTE_EPS = 1e-20
TILES = 4
CHUNK = TILES * P
STEPS = 7

START_TABLE = [
    ["in_stat", "in_aggr", "start_consts", "in_norm", "in_yT", "in_hi", "start_ffn:0", "in_lo", "start_route",
     "in_route", "in_exp", "in_sel:0", "in_sel:1", "in_sel:2", "in_sel:3", "in_sel:4", "in_sel:5", "in_sel:6",
     "in_sel:7", "in_sel:8", "in_sel:9", "in_sel:10"],
]
OPEN_TABLE = [
    ["now_sel:11", "start_ffn:1", "now_sel:12", "ffn_up", "ffn_gated", "now_sel:13", "now_sel:14", "now_wT",
     "in_stat", "ffn_hidden"],
    ["now_wT_copy", "in_aggr", "in_norm", "ffn_up", "ffn_w", "ffn_gated", "ffn_hidden"],
    ["start_fold:0", "ffn_up", "ffn_down", "ffn_w", "in_yT", "ffn_gated", "in_hi", "ffn_hidden"],
    ["start_fold:1", "in_lo", "ffn_down", "ffn_w", "start_fold:2", "ffn_up", "ffn_gated", "ffn_hidden", "in_route"],
    ["ffn_up", "ffn_gated", "ffn_w", "ffn_hidden", "start_att", "in_exp", "in_sel:0", "in_sel:1", "in_sel:2",
     "ffn_down", "in_sel:3"],
    ["ffn_down", "ffn_up", "in_sel:4", "ffn_w", "ffn_gated", "in_sel:5", "ffn_hidden", "in_sel:6"],
    ["ffn_up", "ffn_gated", "in_sel:7", "in_sel:8", "ffn_down", "ffn_w", "ffn_hidden", "in_sel:9", "in_sel:10"],
]
FIRST_TABLE = [
    ["ffn_up", "ffn_gated", "now_sel:11", "out_down", "now_sel:12", "out_copy", "ffn_hidden", "now_sel:13",
     "now_sel:14", "now_wT"],
    ["now_wT_copy", "ffn_up", "ffn_gated", "ffn_w", "ffn_hidden", "out_T", "out_add", "x_copy", "att_stat",
     "att_aggr", "att_norm"],
    ["ffn_w", "ffn_up", "ffn_gated", "ffn_hidden", "ffn_down", "att_hi", "in_stat"],
    ["ffn_up", "ffn_gated", "att_yT", "in_aggr", "in_norm", "ffn_down", "ffn_w", "ffn_hidden", "att_lo"],
    ["ffn_down", "ffn_up", "ffn_w", "att_qkv:0", "att_exp:0", "att_qkv:1", "ffn_gated", "ffn_hidden", "att_feat:0",
     "att_kv:0", "att_exp:1", "att_feat:1", "in_yT"],
    ["ffn_w", "att_kv:1", "att_kv:2", "in_hi", "in_lo", "ffn_up", "ffn_gated", "in_route", "att_kv:3", "in_exp",
     "ffn_down", "in_sel:0", "ffn_hidden", "in_sel:1", "in_sel:2", "in_sel:3"],
    ["att_kv_hi:0", "att_kv_lo:0", "ffn_up", "ffn_gated", "in_sel:4", "in_sel:5", "ffn_w", "in_sel:6", "in_sel:7",
     "in_sel:8", "ffn_hidden", "ffn_down", "in_sel:9", "att_kv_hi:1", "att_kv_lo:1", "in_sel:10"],
]
RAMP_TABLE = [
    ["ffn_up", "now_sel:11", "now_sel:12", "out_down", "ffn_gated", "now_sel:13", "now_sel:14", "ffn_hidden"],
    ["prev_cum:0", "prev_cum_copy:0", "now_wT", "out_copy", "now_wT_copy", "ffn_w", "ffn_up", "prev_mul:0",
     "prev_red:0", "prev_cum:1", "ffn_gated", "ffn_hidden"],
    ["prev_cum_copy:1", "ffn_down", "prev_mul:1", "prev_cum:2", "ffn_up", "ffn_gated", "ffn_w", "ffn_hidden",
     "prev_red:1"],
    ["ffn_up", "ffn_gated", "ffn_w", "ffn_hidden", "prev_cum_copy:2", "prev_mul:2", "ffn_down", "prev_cum:3"],
    ["ffn_up", "prev_red:2", "prev_beta", "ffn_w", "ffn_gated", "prev_cum_copy:3", "prev_mul:3", "prev_red:3",
     "ffn_hidden", "end_div:0", "end_div:1", "end_div:2", "ffn_down", "out_T", "out_add", "x_copy"],
    ["end_oT", "end_o_hi", "ffn_up", "end_o_lo", "ffn_gated", "ffn_w", "ffn_down", "end_proj", "att_stat",
     "end_res", "ffn_hidden"],
    ["att_aggr", "att_norm", "ffn_w", "end_stat", "ffn_up", "ffn_gated", "end_aggr", "ffn_hidden", "att_yT",
     "att_hi", "ffn_down", "att_lo", "att_qkv:0", "att_exp:0", "att_feat:0", "end_norm", "end_zg", "att_kv:0",
     "att_kv:1", "att_qkv:1", "att_exp:1", "att_kv_hi:0", "att_feat:1", "att_kv_lo:0", "att_kv:2", "att_kv:3",
     "end_x2", "att_kv_hi:1", "att_kv_lo:1", "att_cum:0", "att_cum_copy:0", "x2_copy", "att_cum:1",
     "att_cum_copy:1", "in_stat", "in_aggr", "in_norm", "att_mul:0", "in_yT", "in_hi", "att_cum:2",
     "att_cum_copy:2", "in_lo", "att_mul:1", "att_mul:2", "att_red:0", "in_route", "in_exp", "att_red:1",
     "in_sel:0", "att_red:2", "in_sel:1", "in_sel:2", "att_cum:3", "att_cum_copy:3", "in_sel:3", "att_mul:3",
     "in_sel:4", "in_sel:5", "in_sel:6", "in_sel:7", "in_sel:8", "att_red:3", "in_sel:9", "att_beta", "in_sel:10"],
]
Y_TABLE = [
    ["ffn_up", "ffn_gated", "now_sel:11", "now_sel:12", "end_div:0", "ffn_hidden", "end_div:1", "out_down",
     "now_sel:13", "now_sel:14", "now_wT", "end_div:2", "end_oT", "in_stat"],
    ["end_o_hi", "end_o_lo", "out_copy", "now_wT_copy", "ffn_up", "in_aggr", "end_proj", "ffn_gated", "in_norm",
     "out_T", "ffn_w", "end_res", "end_stat", "out_add", "end_aggr", "end_norm", "x_copy", "ffn_hidden"],
    ["ffn_up", "att_stat", "ffn_gated", "att_aggr", "ffn_down", "att_norm", "ffn_w", "in_yT", "in_hi", "in_lo",
     "ffn_hidden"],
    ["ffn_down", "end_zg", "ffn_w", "ffn_up", "ffn_gated", "ffn_hidden", "in_route", "att_yT", "att_hi", "att_lo"],
    ["ffn_up", "end_x2", "ffn_gated", "ffn_down", "att_qkv:0", "in_exp", "in_sel:0", "att_exp:0", "att_feat:0",
     "in_sel:1", "ffn_w", "ffn_hidden", "in_sel:2"],
    ["in_sel:3", "att_qkv:1", "att_kv:0", "att_exp:1", "att_feat:1", "in_sel:4", "ffn_up", "ffn_gated", "ffn_down",
     "ffn_w", "in_sel:5", "att_kv:1", "att_kv:2", "ffn_hidden", "att_kv:3"],
    ["ffn_down", "in_sel:6", "ffn_up", "att_kv_hi:0", "in_sel:7", "att_kv_lo:0", "in_sel:8", "ffn_gated",
     "in_sel:9", "att_kv_hi:1", "att_kv_lo:1", "ffn_w", "ffn_hidden", "in_sel:10"],
]
X_TABLE = [
    ["ffn_up", "now_sel:11", "ffn_gated", "out_down", "out_copy", "now_sel:12", "now_sel:13", "now_sel:14",
     "ffn_hidden", "att_cum:0", "now_wT", "now_wT_copy", "att_cum_copy:0"],
    ["in_stat", "ffn_up", "in_aggr", "in_norm", "att_mul:0", "out_T", "ffn_gated", "att_cum:1", "ffn_w",
     "ffn_hidden"],
    ["out_add", "ffn_up", "ffn_gated", "out_store", "ffn_w", "in_yT", "att_cum_copy:1", "att_mul:1", "ffn_down",
     "ffn_hidden"],
    ["in_hi", "att_cum:2", "x2_copy", "ffn_up", "in_lo", "att_red:0", "ffn_gated", "ffn_w", "ffn_hidden",
     "att_cum_copy:2", "att_mul:2", "att_cum:3", "in_route", "att_red:1", "ffn_down", "att_cum_copy:3"],
    ["in_exp", "ffn_down", "in_sel:0", "in_sel:1", "ffn_up", "ffn_gated", "ffn_w", "ffn_hidden", "in_sel:2",
     "att_red:2", "in_sel:3"],
    ["ffn_up", "ffn_down", "ffn_gated", "in_sel:4", "in_sel:5", "att_mul:3", "in_sel:6", "ffn_w", "ffn_hidden",
     "att_red:3"],
    ["in_sel:7", "ffn_up", "att_beta", "ffn_gated", "in_sel:8", "ffn_w", "in_sel:9", "ffn_hidden", "ffn_down",
     "in_sel:10"],
]
TAIL_TABLE = [
    ["ffn_up", "ffn_gated", "now_sel:11", "ffn_hidden", "end_div:0", "now_sel:12", "end_div:1", "end_div:2",
     "out_down", "out_copy", "now_sel:13", "now_sel:14", "end_oT"],
    ["now_wT", "end_o_hi", "end_o_lo", "ffn_up", "end_proj", "out_T", "ffn_gated", "ffn_w", "now_wT_copy",
     "end_res", "ffn_hidden"],
    ["end_stat", "end_aggr", "ffn_w", "end_norm", "out_add", "att_stat", "att_aggr", "ffn_down", "ffn_up",
     "ffn_gated", "ffn_hidden"],
    ["ffn_up", "ffn_gated", "end_zg", "ffn_w", "ffn_hidden", "end_x2", "in_stat", "ffn_down"],
    ["att_norm", "att_yT", "att_hi", "ffn_up", "att_lo", "in_aggr", "att_qkv:0", "ffn_gated", "ffn_down",
     "att_exp:0", "in_norm", "att_feat:0", "att_qkv:1", "att_kv:0", "ffn_w", "att_kv:1", "ffn_hidden"],
    ["att_exp:1", "att_feat:1", "att_kv:2", "ffn_down", "att_kv:3", "in_yT", "in_hi", "in_lo", "ffn_up",
     "ffn_gated", "ffn_w", "in_route", "in_exp", "in_sel:0", "in_sel:1", "ffn_hidden"],
    ["in_sel:2", "in_sel:3", "att_kv_hi:0", "att_kv_lo:0", "in_sel:4", "in_sel:5", "ffn_up", "in_sel:6",
     "ffn_gated", "in_sel:7", "ffn_w", "in_sel:8", "in_sel:9", "ffn_hidden", "in_sel:10", "att_kv_hi:1",
     "att_kv_lo:1", "ffn_down"],
]
LATE_TABLE = [
    ["ffn_up", "ffn_hidden", "att_cum:0", "att_cum_copy:0", "att_mul:0", "out_down", "ffn_gated", "now_sel:11"],
    ["now_sel:12", "now_sel:13", "out_copy", "now_sel:14", "now_wT", "att_cum:1", "now_wT_copy", "ffn_up",
     "ffn_gated", "ffn_w", "ffn_hidden", "att_cum_copy:1", "att_mul:1"],
    ["ffn_up", "att_cum:2", "ffn_gated", "out_T", "ffn_down", "out_add", "att_cum_copy:2", "ffn_w", "ffn_hidden"],
    ["att_red:0", "ffn_up", "ffn_gated", "ffn_down", "out_store", "att_mul:2", "ffn_w", "ffn_hidden", "att_red:1"],
    ["ffn_up", "ffn_gated", "att_red:2", "x2_copy", "att_cum:3", "ffn_down", "ffn_w", "ffn_hidden"],
    ["ffn_up", "ffn_w", "ffn_gated", "ffn_down", "ffn_hidden", "att_cum_copy:3"],
    ["ffn_w", "att_mul:3", "att_red:3", "end_div:0", "att_beta", "ffn_up", "end_div:1", "ffn_down", "end_div:2",
     "ffn_gated", "end_oT", "end_o_hi", "end_o_lo", "ffn_hidden", "end_proj", "end_res", "end_stat", "end_aggr",
     "end_norm", "end_zg", "end_x2", "in_stat", "in_aggr", "in_norm", "in_yT", "in_hi", "in_lo", "in_route",
     "in_exp", "in_sel:0", "in_sel:1", "in_sel:2", "in_sel:3", "in_sel:4", "in_sel:5", "in_sel:6", "in_sel:7",
     "in_sel:8", "in_sel:9", "in_sel:10"],
]

def broadcast_free(ap, axis, n):
    names = [f"a{i}" for i in range(len(ap.shape))]
    new = names[:axis] + ["z"] + names[axis:]
    if axis < len(names):
        joined = names[:axis] + [f"(z {names[axis]})"] + names[axis + 1:]
    else:
        joined = names[:-1] + [f"({names[-1]} z)"]
    shape = list(ap.shape)
    shape.insert(axis, n)
    return ap.rearrange(f"{' '.join(joined)} -> {' '.join(new)}", z=1).to_broadcast(shape)


def macaron_kernel(nc, x, Wq, bq, Wk, bk, Wv, bv, Wc, We, Wo, bo, gamma, beta,
                   Wr, expert_bias, Wg, Wu, Wd, Wg_s, Wu_s, Wd_s, out):
    B, S, D = x.shape
    KV = Wk.shape[1]
    L = Wc.shape[1]
    E, _, FE = Wg.shape
    FS = Wg_s.shape[1]
    FR = E * FE
    HD = 8
    G = KV // HD
    H = D // HD
    R = H // G
    QKV = D + 2 * KV
    V1 = HD + 1
    KVC = G * HD * V1
    NCH = B * S // CHUNK
    assert D == P and FR % P == 0 and FR // P + 1 == STEPS and S == 2 * P and NCH >= 5

    x_dram = x.rearrange("b s d -> (b s) d").rearrange("(c i p) d -> c p i d", i=TILES, p=P)
    out_dram = out.rearrange("b s d -> (b s) d").rearrange("(c i p) d -> c p i d", i=TILES, p=P)

    with ExitStack() as ctx:
        def sb(name, shape, dt=F32):
            return ctx.enter_context(nc.sbuf_tensor(name, shape, dt))

        def sem(name):
            return ctx.enter_context(nc.semaphore(name))

        wg_raw, wu_raw = sb("wg_raw", [P, FR + FS]), sb("wu_raw", [P, FR + FS])
        wd = sb("wd", [P, STEPS, D])
        wr_raw = sb("wr_raw", [P, E])
        wqkv_raw = sb("wqkv_raw", [P, QKV])
        wkv_in = sb("wkv_in", [P, 2 * KV])
        wo_raw = sb("wo_raw", [P, D])
        wc_in, we_in = sb("wc_in", [KV, L]), sb("we_in", [L, KV])
        bkv_col, bkv_twice = sb("bkv_col", [KV, 2]), sb("bkv_twice", [KV, 2, 2])
        bias_raw = sb("bias_raw", [2, QKV + D])
        gamma_b, beta_b, ebias_b = sb("gamma_b", [P, D]), sb("beta_b", [P, D]), sb("ebias_b", [P, E])
        wg_hi, wg_lo = sb("wg_hi", [P, FR + FS], F32R), sb("wg_lo", [P, FR + FS], F32R)
        wu_hi, wu_lo = sb("wu_hi", [P, FR + FS], F32R), sb("wu_lo", [P, FR + FS], F32R)
        wr_hi, wr_lo = sb("wr_hi", [P, E], F32R), sb("wr_lo", [P, E], F32R)
        wqkv_hi, wqkv_lo = sb("wqkv_hi", [P, QKV], F32R), sb("wqkv_lo", [P, QKV], F32R)
        wo_hi, wo_lo = sb("wo_hi", [P, D], F32R), sb("wo_lo", [P, D], F32R)
        bias_hi, bias_parts = sb("bias_hi", [2, QKV + D], F32R), sb("bias_parts", [2, QKV + D], F32R)
        wcT, wkvT, wce = sb("wcT", [L, KV]), sb("wkvT", [KV, 2, P]), sb("wce", [KV, KV])
        ident, ones, tri = sb("ident", [P, P]), sb("ones", [P, P]), sb("tri", [P, P])
        ones_r, tri_r = sb("ones_r", [P, P], F32R), sb("tri_r", [P, P], F32R)
        ones_rows = sb("ones_rows", [2, P], F32R)
        spread_raw, spread = sb("spread_raw", [2 * E, FR]), sb("spread", [2 * E, FR], F32R)
        iota_e = sb("iota_e", [P, E])
        neg_half = sb("neg_half", [P, TILES])
        x_next, x_cur = sb("x_next", [P, TILES, D]), sb("x_cur", [P, TILES, D])
        x1, x1_beta, x2, x2_cur, y_out = (
            sb(n, [P, TILES, D]) for n in ("x1", "x1_beta", "x2", "x2_cur", "y_out"))
        stats, moments, var_eps, neg_mean, rstd, normed = {}, {}, {}, {}, {}, {}
        for k in "FAZ":
            stats[k], moments[k] = sb(f"stats_{k}", [P, TILES, 6]), sb(f"moments_{k}", [P, TILES, 2])
            var_eps[k], neg_mean[k] = sb(f"var_eps_{k}", [P, TILES]), sb(f"neg_mean_{k}", [P, TILES])
            rstd[k], normed[k] = sb(f"rstd_{k}", [P, TILES]), sb(f"normed_{k}", [P, TILES, D])
        fyT_hi = [sb(f"fyT_hi{i}", [P, CHUNK], F32R) for i in range(2)]
        fyT_lo = [sb(f"fyT_lo{i}", [P, CHUNK], F32R) for i in range(2)]
        exp_neg, denom, score, biased = (sb(n, [P, TILES, E]) for n in ("exp_neg", "denom", "score", "biased"))
        top_val, top_idx = sb("top_val", [P, TILES, 8]), sb("top_idx", [P, TILES, 8], U32)
        is_first, is_second, chosen, picked = (
            sb(n, [P, TILES, E]) for n in ("is_first", "is_second", "chosen", "picked"))
        pick_sum, pick_inv = sb("pick_sum", [P, TILES]), sb("pick_inv", [P, TILES])
        pick_sum_eps = sb("pick_sum_eps", [P, TILES])
        route_w = sb("route_w", [P, TILES, E])
        route_parts = sb("route_parts", [P, TILES, 2 * E], F32R)
        wT = [sb(f"wT{i}", [2 * E, CHUNK], F32R) for i in range(2)]
        silu_g = [sb(f"silu_g{i}", [P, CHUNK]) for i in range(2)]
        gated = [sb(f"gated{i}", [P, CHUNK]) for i in range(2)]
        hidden = sb("hidden", [P, STEPS, CHUNK])
        downT = sb("downT", [P, CHUNK])
        ayT_hi, ayT_lo = sb("ayT_hi", [P, CHUNK], F32R), sb("ayT_lo", [P, CHUNK], F32R)
        qk_exp, qk_relu = sb("qk_exp", [P, TILES, D + KV]), sb("qk_relu", [P, TILES, D + KV])
        qk_feat = sb("qk_feat", [P, TILES, D + KV])
        v_ones = sb("v_ones", [P, TILES, G, V1])
        kv = sb("kv", [P, TILES, KVC])
        kv_hi, kv_lo = sb("kv_hi", [P, TILES, KVC], F32R), sb("kv_lo", [P, TILES, KVC], F32R)
        kv_cum = sb("kv_cum", [P, 2, KVC])
        prod = sb("prod", [P, 2, H * HD * V1])
        num_den = sb("num_den", [P, TILES, H, V1])
        den_eps, den_inv = sb("den_eps", [P, TILES, H]), sb("den_inv", [P, TILES, H])
        att_o = sb("att_o", [P, TILES, D])
        oT_hi, oT_lo = sb("oT_hi", [P, CHUNK], F32R), sb("oT_lo", [P, CHUNK], F32R)
        att_z, z_gamma = sb("att_z", [P, TILES, D]), sb("z_gamma", [P, TILES, D])
        def bank(name):
            return ctx.enter_context(nc.psum_tensor(name, [P, 512], F32))
        ps_gate, ps_up = [bank("ps_gate0"), bank("ps_gate1")], [bank("ps_up0"), bank("ps_up1")]
        ps_w, ps_down, ps_f, ps_a = bank("ps_w"), bank("ps_down"), bank("ps_f"), bank("ps_a")

        fold_loaded, ebias_loaded, att_loaded = sem("fold_loaded"), sem("ebias_loaded"), sem("att_loaded")
        wr_loaded, shared_loaded, routed_loaded, wd_loaded = (
            sem("wr_loaded"), sem("shared_loaded"), sem("routed_loaded"), sem("wd_loaded"))
        x_loaded, x_copied, x2_copied = sem("x_loaded"), sem("x_copied"), sem("x2_copied")
        zeroed, masks_made, consts_made = sem("zeroed"), sem("masks_made"), sem("consts_made")
        dve_consts = sem("dve_consts")
        fold_ready, fold_copied = sem("fold_ready"), sem("fold_copied")
        hi_made, weights_split = sem("hi_made"), sem("weights_split")
        stats_made = {k: sem(f"stats_made_{k}") for k in "FAZ"}
        moments_made = {k: sem(f"moments_made_{k}") for k in "FAZ"}
        eps_added = {k: sem(f"eps_added_{k}") for k in "FAZ"}
        rstd_made = {k: sem(f"rstd_made_{k}") for k in "FAZ"}
        norm_made = {k: sem(f"norm_made_{k}") for k in "FAZ"}
        fyT_ready, fyT_hi_made, fyT_lo_made = sem("fyT_ready"), sem("fyT_hi_made"), sem("fyT_lo_made")
        logits_ready, exp_made, w_made = sem("logits_ready"), sem("exp_made"), sem("w_made")
        sel_chain = [sem("sel_chain0"), sem("sel_chain1")]
        wT_ready, wT_copied = sem("wT_ready"), sem("wT_copied")
        gate_ready, up_ready, silu_made, hidden_made = (
            sem("gate_ready"), sem("up_ready"), sem("silu_made"), sem("hidden_made"))
        gated_made, weight_ready = sem("gated_made"), sem("weight_ready")
        down_ready, down_copied, out_ready, out_added = (
            sem("down_ready"), sem("down_copied"), sem("out_ready"), sem("out_added"))
        ayT_ready, ayT_hi_made, ayT_lo_made = sem("ayT_ready"), sem("ayT_hi_made"), sem("ayT_lo_made")
        qkv_ready, qkv_read, feat_made = sem("qkv_ready"), sem("qkv_read"), sem("feat_made")
        kv_made, cum_ready, cum_copied, red_made = (
            sem("kv_made"), sem("cum_ready"), sem("cum_copied"), sem("red_made"))
        kv_hi_made, kv_lo_made = sem("kv_hi_made"), sem("kv_lo_made")
        prod_made = [sem("prod_made0"), sem("prod_made1")]
        den_chain, o_made = sem("den_chain"), sem("o_made")
        oT_ready, oT_hi_made, oT_lo_made = sem("oT_ready"), sem("oT_hi_made"), sem("oT_lo_made")
        z_ready, z_added, z_scaled, x2_made, beta_added = (
            sem("z_ready"), sem("z_added"), sem("z_scaled"), sem("x2_made"), sem("beta_added"))
        out_stored = sem("out_stored")

        waits_passed = sem("waits_passed")

        SEL_CHAIN = 2 * STEPS

        def slot1(c):
            return c if isinstance(c, int) and c < 2 else 2 * c - 2

        def slot2(c):
            return c + NCH if isinstance(c, int) and c >= NCH - 2 else 2 * c + 3

        def need(eng, semaphore, value):
            if not isinstance(value, int) or value > 0:
                eng.wait_ge(semaphore, value)

        def need_apart(eng, semaphore, value):
            if not isinstance(value, int) or value > 0:
                eng.wait_ge(semaphore, value).then_inc(waits_passed, 1)

        def vector_multiplies(c):
            return isinstance(c, int) and c in (0, 1, NCH - 1)

        def multiply_features(eng, c, i):
            need(eng, cum_copied, TILES * c + i + 1)
            need(eng, red_made, TILES * c + i - 1)
            for g in range(G):
                qf = qk_feat[:, i, g * R * HD:(g + 1) * R * HD].rearrange("p (r f) -> p r f", r=R)
                cum = kv_cum[:, i % 2, g * HD * V1:(g + 1) * HD * V1].rearrange("p (f v) -> p f v", f=HD)
                dst = prod[:, i % 2, g * R * HD * V1:(g + 1) * R * HD * V1]
                last = eng.tensor_tensor(dst.rearrange("p (r f v) -> p r f v", r=R, f=HD),
                                         broadcast_free(qf, 3, V1), broadcast_free(cum, 1, R), ALU.mult)
            last.then_inc(prod_made[i % 2], 1)

        def walk(eng, do):
            def entry(name, args):
                name, *number = name.split(":")
                if name in do:
                    do[name](*args, *map(int, number))

            def ffn_args(which, c):
                slot = slot1(c) if which == 1 else slot2(c)
                return slot, slot % 2 if isinstance(slot, int) else which - 1, which, c

            def run(ffn, table, args):
                for m in range(len(table)):
                    for name in table[m]:
                        kind = name.split("_")[0]
                        if kind == "ffn" and ffn is not None:
                            entry(name, (ffn[0], ffn[1], m, (ffn[1] + m) % 2))
                        elif kind == "now" and ffn is not None:
                            entry(name.replace("now", "in"), ffn)
                        elif kind == "prev" and kind in args:
                            entry(name.replace("prev", "att"), args[kind])
                        elif kind in args:
                            entry(name, args[kind])

            def slot_y(n):
                run(ffn_args(2, n - 2), Y_TABLE, {"out": ffn_args(1, n), "att": (n,), "end": (n - 1,), "x": (n + 1,),
                                                  "in": ffn_args(1, n + 1)})

            def slot_x(n):
                run(ffn_args(1, n), X_TABLE, {"out": ffn_args(2, n - 3), "att": (n - 1,), "x2": (n - 2,),
                                              "in": ffn_args(2, n - 2)})

            entry("x_copy", (0,))
            run(None, START_TABLE, {"start": (), "in": ffn_args(1, 0)})
            run(ffn_args(1, 0), OPEN_TABLE, {"start": (), "in": ffn_args(1, 1)})
            run(ffn_args(1, 1), FIRST_TABLE, {"out": ffn_args(1, 0), "att": (0,), "x": (1,), "in": ffn_args(1, 2)})
            run(ffn_args(1, 2), RAMP_TABLE, {"prev": (0,), "out": ffn_args(1, 1), "end": (0,), "att": (1,), "x": (2,),
                                             "x2": (0,), "in": ffn_args(2, 0)})
            slot_y(2)
            slot_x(3)
            with eng.Fori(3, NCH - 1) as n:
                slot_y(n)
                slot_x(n + 1)
            last = NCH - 1
            run(ffn_args(2, last - 2), TAIL_TABLE,
                {"out": ffn_args(1, last), "end": (last - 1,), "att": (last,), "in": ffn_args(2, last - 1)})
            run(ffn_args(2, last - 1), LATE_TABLE,
                {"out": ffn_args(2, last - 2), "att": (last,), "x2": (last - 1,), "end": (last,),
                 "in": ffn_args(2, last)})
            run(ffn_args(2, last), X_TABLE, {"out": ffn_args(2, last - 1), "x2": (last,)})
            run(None, X_TABLE, {"out": ffn_args(2, last)})

        block = ctx.enter_context(nc.Block())

        @block.sync
        def _(sp):
            sp.dma_start(x_next[:], x_dram[0]).then_inc(x_loaded, 16)
            for dst, src in ((wc_in[:], Wc), (wkv_in[:, 0:KV], Wk), (wkv_in[:, KV:2 * KV], Wv), (we_in[:], We),
                             (bkv_col[:, 0:1], bk.rearrange("(p a) -> p a", a=1)),
                             (bkv_col[:, 1:2], bv.rearrange("(p a) -> p a", a=1))):
                sp.dma_start(dst, src).then_inc(fold_loaded, 16)
            sp.dma_start(ebias_b[:], expert_bias.rearrange("(a d) -> a d", a=1).to_broadcast([P, E])
                         ).then_inc(ebias_loaded, 16)
            sp.dma_start(wd[0:FS, 0, :], Wd_s).then_inc(wd_loaded, 16)
            sp.dma_start(wd[:, 1:STEPS, :],
                         Wd.rearrange("e f d -> (e f) d").rearrange("(m p) d -> p m d", p=P)).then_inc(wd_loaded, 16)
            for dst, src in ((wqkv_raw[:, 0:D], Wq), (wo_raw[:], Wo),
                             (bias_raw[:, 0:D], bq.rearrange("(a d) -> a d", a=1).to_broadcast([2, D])),
                             (bias_raw[:, QKV:QKV + D], bo.rearrange("(a d) -> a d", a=1).to_broadcast([2, D])),
                             (gamma_b[:], gamma.rearrange("(a d) -> a d", a=1).to_broadcast([P, D])),
                             (beta_b[:], beta.rearrange("(a d) -> a d", a=1).to_broadcast([P, D]))):
                sp.dma_start(dst, src).then_inc(att_loaded, 16)

            def x_load(c):
                need_apart(sp, x_copied, c)
                need_apart(sp, norm_made["F"], slot1(c - 1) + 1)
                sp.dma_start(x_next[:], x_dram[c]).then_inc(x_loaded, 16)

            x_load(1)
            x_load(2)
            with sp.Fori(3, NCH) as c:
                x_load(c)
            sp.wait_ge(out_stored, 16 * NCH)

        @block.gpsimd
        def _(pool):
            pool.memset(ident[:], 0.0)
            pool.memset(ones[:], 1.0)
            pool.memset(spread_raw[:], 0.0)
            pool.memset(neg_half[:], -0.5).then_inc(zeroed, 1)
            pool.wait_ge(zeroed, 1)
            pool.affine_select(out=ident[:], in_=ident[:], compare_op=ALU.not_equal, fill=1.0, base=0,
                               pattern=[[-1, P]], channel_multiplier=1)
            pool.affine_select(out=tri[:], in_=ones[:], compare_op=ALU.is_ge, fill=0.0, base=0,
                               pattern=[[1, P]], channel_multiplier=-1)
            pool.affine_select(out=spread_raw[:], in_=spread_raw[:], compare_op=ALU.not_equal, fill=1.0, base=0,
                               pattern=[[-1, E], [0, FE]], channel_multiplier=1).then_inc(zeroed, 1)
            pool.wait_ge(zeroed, 2)
            pool.affine_select(out=spread_raw[:], in_=spread_raw[:], compare_op=ALU.not_equal, fill=1.0, base=-E,
                               pattern=[[-1, E], [0, FE]], channel_multiplier=1).then_inc(masks_made, 1)

            def normalise(k, slot, source, free):
                need_apart(pool, moments_made[k], slot + 1)
                pool.tensor_scalar(var_eps[k][:], moments[k][:, :, 1], 1.0, LN_EPS, ALU.mult, ALU.add)
                pool.tensor_scalar(neg_mean[k][:], moments[k][:, :, 0], -1.0, 0.0, ALU.mult, ALU.add
                                   ).then_inc(eps_added[k], 1)
                need(pool, eps_added[k], slot + 1)
                pool.tensor_tensor(rstd[k][:], var_eps[k][:], neg_half[:], ALU.pow).then_inc(rstd_made[k], 1)
                free()
                need_apart(pool, rstd_made[k], slot + 1)
                for i in range(TILES):
                    last = pool.tensor_scalar(normed[k][:, i, :], source[:, i, :], neg_mean[k][:, i:i + 1],
                                              rstd[k][:, i:i + 1], ALU.add, ALU.mult)
                last.then_inc(norm_made[k], 1)

            def in_norm(slot, copy, which, c):
                def free():
                    need(pool, fyT_ready, slot)
                normalise("F", slot, x_next if which == 1 else x2, free)

            def att_norm(c):
                def free():
                    need(pool, z_added, c)
                normalise("A", c, x1, free)

            def att_beta(c):
                need(pool, x2_made, c)
                need(pool, out_added, slot1(c) + 1)
                pool.tensor_tensor(x1_beta[:], x1[:], broadcast_free(beta_b[:], 1, TILES), ALU.add
                                   ).then_inc(beta_added, 1)

            def end_norm(c):
                def free():
                    need(pool, z_scaled, c)
                normalise("Z", c, att_z, free)

            def att_kv(c, i):
                need(pool, feat_made, 2 * c + i // 2 + 1)
                if i == 0:
                    need(pool, kv_hi_made, 2 * c)
                key = qk_feat[:, i, D:D + KV].rearrange("p (g f) -> p g f", g=G)
                pool.tensor_tensor(kv[:, i, :].rearrange("p (g f v) -> p g f v", g=G, f=HD),
                                   broadcast_free(key, 3, V1), broadcast_free(v_ones[:, i], 2, HD), ALU.mult
                                   ).then_inc(kv_made, 1)

            def att_kv_lo(c, j):
                t = slice(2 * j, 2 * j + 2)
                need(pool, kv_hi_made, 2 * c + j + 1)
                if j == 0:
                    need(pool, cum_ready, TILES * c)
                pool.tensor_tensor(kv_lo[:, t, :], kv[:, t, :], kv_hi[:, t, :].bitcast(F32), ALU.subtract
                                   ).then_inc(kv_lo_made, 1)

            def att_mul(c, i):
                if not (i % 2 and vector_multiplies(c)):
                    multiply_features(pool, c, i)

            def start_att():
                pool.wait_ge(att_loaded, 16 * 6)

            walk(pool, {"start_att": start_att, "in_norm": in_norm, "att_norm": att_norm, "end_norm": end_norm,
                        "att_beta": att_beta, "att_kv": att_kv, "att_kv_lo": att_kv_lo, "att_mul": att_mul})

        @block.scalar
        def _(act):
            act.dma_start(wr_raw[:], Wr).then_inc(wr_loaded, 16)
            act.dma_start(wg_raw[:, 0:FS], Wg_s).then_inc(shared_loaded, 16)
            act.dma_start(wu_raw[:, 0:FS], Wu_s).then_inc(shared_loaded, 16)
            act.dma_start(wg_raw[:, FS:FS + FR].rearrange("p (e f) -> p e f", e=E), Wg.rearrange("e d f -> d e f")
                          ).then_inc(routed_loaded, 16)
            act.dma_start(wu_raw[:, FS:FS + FR].rearrange("p (e f) -> p e f", e=E), Wu.rearrange("e d f -> d e f")
                          ).then_inc(routed_loaded, 16)

            def start_route():
                act.wait_ge(wr_loaded, 16)
                act.copy(wr_hi[:], wr_raw[:]).then_inc(hi_made, 1)

            def start_ffn(k):
                act.wait_ge((shared_loaded, routed_loaded)[k], 32)
                f = (slice(0, FS), slice(FS, FS + FR))[k]
                act.copy(wg_hi[:, f], wg_raw[:, f]).then_inc(hi_made, 1)
                act.copy(wu_hi[:, f], wu_raw[:, f]).then_inc(hi_made, 1)

            def start_att():
                act.wait_ge(att_loaded, 16 * 6)
                act.wait_ge(fold_copied, 4)
                act.copy(wqkv_hi[:], wqkv_raw[:]).then_inc(hi_made, 1)
                act.copy(wo_hi[:], wo_raw[:]).then_inc(hi_made, 1)
                act.copy(bias_hi[:], bias_raw[:]).then_inc(hi_made, 1)

            def x_copy(c):
                need(act, x_loaded, 16 * (c + 1))
                need(act, out_added, slot1(c - 1) + 1 if not (isinstance(c, int) and c == 0) else 0)
                act.copy(x_cur[:], x_next[:]).then_inc(x_copied, 1)

            def out_store(slot, copy, which, c):
                if which == 2:
                    need(act, out_added, slot + 1)
                    act.dma_start(out_dram[c], y_out[:]).then_inc(out_stored, 16)

            def x2_copy(c):
                need(act, x2_made, c + 1)
                if not (isinstance(c, int) and c == 0):
                    need(act, out_added, slot2(c - 1) + 1)
                act.copy(x2_cur[:], x2[:]).then_inc(x2_copied, 1)

            def in_hi(slot, copy, which, c):
                need(act, fyT_ready, slot + 1)
                act.copy(fyT_hi[copy][:], ps_f[:]).then_inc(fyT_hi_made, 1)

            def in_exp(slot, copy, which, c):
                need(act, logits_ready, slot + 1)
                need(act, w_made, slot)
                act.activation(exp_neg[:], ps_f[:, 0:TILES * E].rearrange("p (i e) -> p i e", e=E), ACT.Exp,
                               scale=-1.0).then_inc(exp_made, 1)

            def in_wT_copy(slot, copy, which, c):
                need(act, wT_ready, slot + 1)
                act.copy(wT[copy][:], ps_f[0:2 * E, :]).then_inc(wT_copied, 1)

            def ffn_up(slot, copy, m, b):
                rows = P if m > 0 else FS
                need(act, gate_ready, STEPS * slot + m + 1)
                need(act, hidden_made, STEPS * slot + m - 1)
                act.activation(silu_g[b][0:rows, :], ps_gate[b][0:rows, :], ACT.Silu).then_inc(silu_made, 1)

            def out_copy(slot, copy, which, c):
                need(act, down_ready, slot + 1)
                need(act, out_ready, slot)
                act.copy(downT[:], ps_down[:]).then_inc(down_copied, 1)

            def att_hi(c):
                need(act, ayT_ready, c + 1)
                act.copy(ayT_hi[:], ps_a[:]).then_inc(ayT_hi_made, 1)

            def att_exp(c, j):
                t = slice(2 * j, 2 * j + 2)
                need(act, qkv_ready, 2 * c + j + 1)
                if j == 0:
                    need(act, feat_made, 2 * c)
                    need(act, kv_made, TILES * c)
                src = (ps_a, ps_f)[j][:, 0:2 * QKV].rearrange("p (i q) -> p i q", i=2)
                act.activation(qk_exp[:, t, :], src[:, :, 0:D + KV], ACT.Exp)
                act.activation(qk_relu[:, t, :], src[:, :, 0:D + KV], ACT.Relu)
                for i in range(2):
                    last = act.copy(v_ones[:, 2 * j + i, :, 0:HD],
                                    src[:, i, D + KV:QKV].rearrange("p (g v) -> p g v", g=G))
                last.then_inc(qkv_read, 1)

            def att_kv_hi(c, j):
                t = slice(2 * j, 2 * j + 2)
                need(act, kv_made, TILES * c + 2 * j + 2)
                if j == 0:
                    need(act, cum_ready, TILES * c)
                act.copy(kv_hi[:, t, :], kv[:, t, :]).then_inc(kv_hi_made, 1)

            def att_cum_copy(c, i):
                need(act, cum_ready, TILES * c + i + 1)
                need(act, prod_made[i % 2], 2 * c + i // 2)
                act.copy(kv_cum[:, i % 2, :], ps_a[:, 0:KVC]).then_inc(cum_copied, 1)

            def end_o_hi(c):
                need(act, oT_ready, c + 1)
                act.copy(oT_hi[:], ps_a[:]).then_inc(oT_hi_made, 1)

            walk(act, {"start_route": start_route, "start_ffn": start_ffn, "start_att": start_att, "x_copy": x_copy,
                       "x2_copy": x2_copy, "out_store": out_store, "in_hi": in_hi, "in_exp": in_exp,
                       "in_wT_copy": in_wT_copy, "ffn_up": ffn_up, "out_copy": out_copy, "att_hi": att_hi,
                       "att_exp": att_exp, "att_kv_hi": att_kv_hi, "att_cum_copy": att_cum_copy,
                       "end_o_hi": end_o_hi})

        @block.vector
        def _(dve):
            dve.memset(v_ones[:], 1.0).then_inc(dve_consts, 1)
            for e in range(E):
                last = dve.memset(iota_e[:, e:e + 1], float(e))
            last.then_inc(dve_consts, 1)

            def start_consts():
                dve.wait_ge(masks_made, 1)
                dve.tensor_copy(spread[:], spread_raw[:])
                dve.tensor_copy(ones_r[:], ones[:])
                dve.tensor_copy(tri_r[:], tri[:])
                dve.tensor_copy(ones_rows[:], ones[0:2, :]).then_inc(consts_made, 1)

            def start_fold(k):
                dve.wait_ge(fold_ready, k + 1)
                if k == 0:
                    dve.tensor_copy(bkv_twice[:], broadcast_free(bkv_col[:], 2, 2))
                    dve.tensor_copy(wcT[:], ps_a[0:L, 0:KV])
                    dve.tensor_copy(wkvT[:], ps_a[0:KV, P:3 * P].rearrange("p (a b) -> p a b", a=2)
                                    ).then_inc(fold_copied, 1)
                if k == 1:
                    dve.tensor_copy(wce[:], ps_a[0:KV, 0:KV]).then_inc(fold_copied, 1)
                if k == 2:
                    dve.tensor_copy(wqkv_raw[:, D:QKV], ps_a[:, 0:2 * KV]).then_inc(fold_copied, 1)
                    dve.tensor_copy(bias_raw[:, D:QKV], ps_a[0:2, 2 * KV:4 * KV]).then_inc(fold_copied, 1)

            def low_part(n, lo, hi, raw):
                dve.wait_ge(hi_made, n)
                dve.tensor_tensor(lo, raw, hi.bitcast(F32), ALU.subtract).then_inc(weights_split, 1)

            def start_route():
                low_part(3, wr_lo[:], wr_hi[:], wr_raw[:])
                dve.wait_ge(ebias_loaded, 16)

            def start_ffn(k):
                f = (slice(0, FS), slice(FS, FS + FR))[k]
                low_part(1 + 3 * k, wg_lo[:, f], wg_hi[:, f], wg_raw[:, f])
                low_part(2 + 3 * k, wu_lo[:, f], wu_hi[:, f], wu_raw[:, f])

            def start_att():
                dve.wait_ge(att_loaded, 16 * 6)
                for n, (lo, hi, raw) in enumerate(((wqkv_lo, wqkv_hi, wqkv_raw), (wo_lo, wo_hi, wo_raw),
                                                   (bias_parts, bias_hi, bias_raw))):
                    low_part(6 + n, lo[:], hi[:], raw[:])
                dve.wait_ge(weights_split, 8)
                dve.tensor_copy(bias_parts[0:1, :], bias_hi[0:1, :].bitcast(F32)).then_inc(weights_split, 1)

            def statistics(k, slot, source):
                for i in range(TILES):
                    last = dve.bn_stats(stats[k][:, i, :], source[:, i, :])
                last.then_inc(stats_made[k], 1)

            def aggregate(k, slot):
                need(dve, stats_made[k], slot + 1)
                need_apart(dve, norm_made[k], slot)
                for i in range(TILES):
                    last = dve.bn_aggr(moments[k][:, i, :], stats[k][:, i, :])
                last.then_inc(moments_made[k], 1)

            def in_stat(slot, copy, which, c):
                if which == 1:
                    need(dve, x_loaded, 16 * (c + 1))
                    statistics("F", slot, x_next)
                else:
                    need(dve, x2_made, c + 1)
                    statistics("F", slot, x2)

            def in_aggr(slot, copy, which, c):
                aggregate("F", slot)

            def in_lo(slot, copy, which, c):
                need(dve, fyT_hi_made, slot + 1)
                dve.tensor_tensor(fyT_lo[copy][:], ps_f[:], fyT_hi[copy][:].bitcast(F32), ALU.subtract
                                  ).then_inc(fyT_lo_made, 1)

            def in_sel(slot, copy, which, c, k):
                wait = need_apart if k in (3, 4) else need
                if k > 0:
                    before = k - 1 - (k == 6)
                    wait(dve, sel_chain[before // STEPS], STEPS * slot + before % STEPS + 1)
                if k == 0:
                    need(dve, exp_made, slot + 1)
                    need(dve, wT_ready, slot)
                    ins = dve.tensor_scalar(denom[:], exp_neg[:], 1.0, None, ALU.add)
                if k == 1:
                    ins = dve.reciprocal(score[:], denom[:])
                if k == 2:
                    ins = dve.tensor_tensor(biased[:], score[:], broadcast_free(ebias_b[:], 1, TILES), ALU.add)
                if k == 3:
                    for i in range(TILES):
                        ins = dve.max(top_val[:, i, :], biased[:, i, :])
                if k == 4:
                    for i in range(TILES):
                        ins = dve.max_index(top_idx[:, i, :], top_val[:, i, :], biased[:, i, :])
                if k in (5, 6):
                    ins = dve.tensor_tensor((is_first, is_second)[k - 5][:], broadcast_free(iota_e[:], 1, TILES),
                                            top_idx[:, :, k - 5:k - 4].to_broadcast([P, TILES, E]), ALU.is_equal)
                if k == 7:
                    ins = dve.tensor_tensor(chosen[:], is_first[:], is_second[:], ALU.add)
                if k == 8:
                    ins = dve.tensor_tensor(picked[:], score[:], chosen[:], ALU.mult)
                if k == 9:
                    ins = dve.tensor_reduce(pick_sum[:], picked[:], AX_X, ALU.add)
                if k == 10:
                    ins = dve.tensor_scalar(pick_sum_eps[:], pick_sum[:], ROUTE_EPS, None, ALU.add)
                if k == 11:
                    ins = dve.reciprocal(pick_inv[:], pick_sum_eps[:])
                if k == 12:
                    ins = dve.tensor_tensor(route_w[:], picked[:], broadcast_free(pick_inv[:], 2, E), ALU.mult)
                if k == 13:
                    ins = dve.tensor_copy(route_parts[:, :, 0:E], route_w[:])
                if k == SEL_CHAIN:
                    dve.tensor_tensor(route_parts[:, :, E:2 * E], route_w[:], route_parts[:, :, 0:E].bitcast(F32),
                                      ALU.subtract).then_inc(w_made, 1)
                else:
                    ins.then_inc(sel_chain[k // STEPS], 1)

            def ffn_gated(slot, copy, m, b):
                routed = m > 0
                rows = P if routed else FS
                need(dve, silu_made, STEPS * slot + m + 1)
                need(dve, up_ready, STEPS * slot + m + 1)
                if routed:
                    dve.tensor_tensor(gated[b][:], silu_g[b][:], ps_up[b][:], ALU.mult
                                      ).then_inc(gated_made, 2 if m == 1 else 1)
                else:
                    dve.tensor_tensor(hidden[0:rows, m, :], silu_g[b][0:rows, :], ps_up[b][0:rows, :], ALU.mult
                                      ).then_inc(hidden_made, 1)

            def ffn_hidden(slot, copy, m, b):
                if m > 0:
                    need(dve, gated_made, STEPS * slot + m + 1)
                    need(dve, weight_ready, STEPS * slot + m + 1)
                    dve.tensor_tensor(hidden[:, m, :], gated[b][:], ps_w[:], ALU.mult).then_inc(hidden_made, 1)

            def out_add(slot, copy, which, c):
                need(dve, out_ready, slot + 1)
                if which == 1:
                    need(dve, x_copied, c + 1)
                    need(dve, beta_added, c)
                    src, dst = x_cur, x1
                else:
                    need(dve, x2_copied, c + 1)
                    need(dve, out_stored, 16 * c)
                    src, dst = x2_cur, y_out
                dve.scalar_tensor_tensor(out=dst[:], in0=ps_f[:].rearrange("p (i d) -> p i d", i=TILES), scalar=0.5,
                                         in1=src[:], op0=ALU.mult, op1=ALU.add).then_inc(out_added, 1)

            def att_stat(c):
                need(dve, out_added, slot1(c) + 1)
                statistics("A", c, x1)

            def att_aggr(c):
                aggregate("A", c)

            def att_lo(c):
                need(dve, ayT_hi_made, c + 1)
                dve.tensor_tensor(ayT_lo[:], ps_a[:], ayT_hi[:].bitcast(F32), ALU.subtract).then_inc(ayT_lo_made, 1)

            def att_feat(c, j):
                t = slice(2 * j, 2 * j + 2)
                need(dve, qkv_read, 2 * c + j + 1)
                if j == 0:
                    need(dve, prod_made[0], 2 * c)
                    need(dve, prod_made[1], 2 * c)
                dve.scalar_tensor_tensor(out=qk_feat[:, t, :], in0=qk_exp[:, t, :], scalar=1.0,
                                         in1=qk_relu[:, t, :], op0=ALU.min, op1=ALU.add).then_inc(feat_made, 1)

            def att_red(c, i):
                if i % 2 and vector_multiplies(c):
                    multiply_features(dve, c, i)
                need(dve, prod_made[i % 2], 2 * c + i // 2 + 1)
                dve.tensor_reduce(num_den[:, i], prod[:, i % 2, :].rearrange("p (h f v) -> p h v f", h=H, f=HD),
                                  AX_X, ALU.add).then_inc(red_made, 1)

            def end_div(c, k):
                if k == 0:
                    need(dve, red_made, TILES * (c + 1))
                    dve.tensor_scalar(den_eps[:], num_den[:, :, :, HD], DEN_EPS, None, ALU.add).then_inc(den_chain, 1)
                if k == 1:
                    need(dve, den_chain, 2 * c + 1)
                    dve.reciprocal(den_inv[:], den_eps[:]).then_inc(den_chain, 1)
                if k == 2:
                    need(dve, den_chain, 2 * c + 2)
                    need(dve, oT_ready, c)
                    dve.tensor_tensor(att_o[:].rearrange("p i (h v) -> p i h v", h=H), num_den[:, :, :, 0:HD],
                                      broadcast_free(den_inv[:], 3, HD), ALU.mult).then_inc(o_made, 1)

            def end_o_lo(c):
                need(dve, oT_hi_made, c + 1)
                dve.tensor_tensor(oT_lo[:], ps_a[:], oT_hi[:].bitcast(F32), ALU.subtract).then_inc(oT_lo_made, 1)

            def end_res(c):
                need(dve, z_ready, c + 1)
                need(dve, norm_made["Z"], c)
                dve.tensor_tensor(att_z[:], ps_a[:].rearrange("p (i d) -> p i d", i=TILES), normed["A"][:], ALU.add
                                  ).then_inc(z_added, 1)

            def end_stat(c):
                need(dve, z_added, c + 1)
                statistics("Z", c, att_z)

            def end_aggr(c):
                aggregate("Z", c)

            def end_zg(c):
                need(dve, norm_made["Z"], c + 1)
                dve.tensor_tensor(z_gamma[:], normed["Z"][:], broadcast_free(gamma_b[:], 1, TILES), ALU.mult
                                  ).then_inc(z_scaled, 1)

            def end_x2(c):
                need(dve, z_scaled, c + 1)
                need(dve, beta_added, c + 1)
                need(dve, x2_copied, c)
                if not (isinstance(c, int) and c == 0):
                    need(dve, norm_made["F"], slot2(c - 1) + 1)
                dve.tensor_tensor(x2[:], z_gamma[:], x1_beta[:], ALU.add).then_inc(x2_made, 1)

            walk(dve, {"start_consts": start_consts, "start_fold": start_fold, "start_route": start_route,
                       "start_ffn": start_ffn, "start_att": start_att, "in_stat": in_stat, "in_aggr": in_aggr,
                       "att_aggr": att_aggr, "end_stat": end_stat, "end_aggr": end_aggr, "end_zg": end_zg,
                       "in_lo": in_lo, "in_sel": in_sel, "ffn_gated": ffn_gated, "ffn_hidden": ffn_hidden,
                       "out_add": out_add, "att_stat": att_stat, "att_lo": att_lo, "att_feat": att_feat,
                       "att_red": att_red, "end_div": end_div, "end_o_lo": end_o_lo, "end_res": end_res,
                       "end_x2": end_x2})

        @block.tensor
        def _(pe):
            def start_fold(k):
                if k == 0:
                    pe.wait_ge(masks_made, 1)
                    pe.wait_ge(fold_loaded, 16 * 6)
                    pe.transpose(ps_a[0:L, 0:KV], wc_in[:], ident[0:KV, 0:KV])
                    for j in range(2):
                        last = pe.transpose(ps_a[0:KV, (1 + j) * P:(2 + j) * P], wkv_in[:, j * KV:(j + 1) * KV],
                                            ident[:])
                if k == 1:
                    pe.wait_ge(fold_copied, 1)
                    last = pe.matmul(ps_a[0:KV, 0:KV], wcT[:], we_in[:], start=True, stop=True)
                if k == 2:
                    pe.wait_ge(fold_copied, 2)
                    for j in range(2):
                        pe.matmul(ps_a[:, j * KV:(j + 1) * KV], wkvT[:, j, :], wce[:], start=True, stop=True)
                    for j in range(2):
                        last = pe.matmul(ps_a[0:2, (2 + j) * KV:(3 + j) * KV], bkv_twice[:, j, :], wce[:],
                                         start=True, stop=True)
                last.then_inc(fold_ready, 1)

            def first_use(slot, m, semaphore, value):
                if isinstance(slot, int) and slot == 0 and m < 2:
                    pe.wait_ge(semaphore, value)

            def in_yT(slot, copy, which, c):
                need(pe, norm_made["F"], slot + 1)
                need(pe, out_added, slot - 1)
                if isinstance(slot, int) and slot in (2, 3):
                    need(pe, qkv_read, 2 * (slot - 1))
                if isinstance(slot, int) and slot == 2 * NCH - 2:
                    need(pe, qkv_read, 2 * NCH)
                if isinstance(slot, int) and slot == 0:
                    pe.wait_ge(masks_made, 1)
                for i in range(TILES):
                    last = pe.transpose(ps_f[:, i * P:(i + 1) * P], normed["F"][:, i, :], ident[:])
                last.then_inc(fyT_ready, 1)

            def in_route(slot, copy, which, c):
                need(pe, fyT_lo_made, slot + 1)
                first_use(slot, 0, weights_split, 3)
                for i in range(TILES):
                    dst, t = ps_f[:, i * E:(i + 1) * E], slice(i * P, (i + 1) * P)
                    pe.matmul(dst, fyT_hi[copy][:, t], wr_hi[:], start=True, stop=False)
                    pe.matmul(dst, fyT_hi[copy][:, t], wr_lo[:], start=False, stop=False)
                    last = pe.matmul(dst, fyT_lo[copy][:, t], wr_hi[:], start=False, stop=True)
                last.then_inc(logits_ready, 1)

            def in_wT(slot, copy, which, c):
                need(pe, w_made, slot + 1)
                if which == 1 and not (isinstance(c, int) and c <= 2):
                    need(pe, qkv_read, 2 * c)
                for i in range(TILES):
                    last = pe.transpose(ps_f[0:2 * E, i * P:(i + 1) * P], route_parts[:, i, :].bitcast(F32), ident[:])
                last.then_inc(wT_ready, 1)

            def down(slot, m):
                rows = P if m > 0 else FS
                need(pe, hidden_made, STEPS * slot + m + 1)
                if m == 0:
                    need(pe, down_copied, slot)
                    first_use(slot, m, wd_loaded, 16 * 2)
                last = pe.matmul(ps_down[:], wd[0:rows, m, :], hidden[0:rows, m, :], start=(m == 0),
                                 stop=(m == STEPS - 1))
                if m == STEPS - 1:
                    last.then_inc(down_ready, 1)

            def split_matmul(dst, w_hi, w_lo, y_hi, y_lo):
                pe.matmul(dst, w_hi, y_hi, start=True, stop=False)
                pe.matmul(dst, w_hi, y_lo, start=False, stop=False)
                return pe.matmul(dst, w_lo, y_hi, start=False, stop=True)

            def ffn_up(slot, copy, m, b):
                rows = P if m > 0 else FS
                f = slice(0, FS) if m == 0 else slice(FS + (m - 1) * P, FS + m * P)
                t = STEPS * slot + m
                if m == 0:
                    need(pe, fyT_lo_made, slot + 1)
                first_use(slot, m, weights_split, 2 + 3 * m)
                need(pe, silu_made, t - 1)
                split_matmul(ps_gate[b][0:rows, :], wg_hi[:, f], wg_lo[:, f], fyT_hi[copy][:], fyT_lo[copy][:]
                             ).then_inc(gate_ready, 1)
                if m == 2:
                    need(pe, hidden_made, t - 1)
                else:
                    need(pe, gated_made, t - 1)
                split_matmul(ps_up[b][0:rows, :], wu_hi[:, f], wu_lo[:, f], fyT_hi[copy][:], fyT_lo[copy][:]
                             ).then_inc(up_ready, 1)

            def ffn_down(slot, copy, m, b):
                down(slot, m - 2)

            def ffn_w(slot, copy, m, b):
                if m == 1:
                    need(pe, wT_copied, slot + 1)
                    first_use(slot, m, consts_made, 1)
                need(pe, hidden_made, STEPS * slot + m)
                pe.matmul(ps_w[:], spread[:, (m - 1) * P:m * P], wT[copy][:], start=True, stop=True
                          ).then_inc(weight_ready, 2 if m == 1 else 1)

            def out_down(slot, copy, which, c):
                down(slot, STEPS - 2)
                down(slot, STEPS - 1)

            def out_T(slot, copy, which, c):
                need(pe, down_copied, slot + 1)
                need(pe, wT_copied, slot + 1 if isinstance(slot, int) and slot == 2 * NCH - 1 else slot + 2)
                for i in range(TILES):
                    last = pe.transpose(ps_f[:, i * P:(i + 1) * P], downT[:, i * P:(i + 1) * P], ident[:])
                last.then_inc(out_ready, 1)

            def att_yT(c):
                need(pe, norm_made["A"], c + 1)
                need(pe, z_added, c)
                for i in range(TILES):
                    last = pe.transpose(ps_a[:, i * P:(i + 1) * P], normed["A"][:, i, :], ident[:])
                last.then_inc(ayT_ready, 1)

            def bias_and_split(dst, y_hi, y_lo, w_hi, w_lo, cols):
                pe.matmul(dst, ones_rows[:], bias_parts[:, cols], start=True, stop=False)
                pe.matmul(dst, y_hi, w_hi[:], start=False, stop=False)
                pe.matmul(dst, y_hi, w_lo[:], start=False, stop=False)
                return pe.matmul(dst, y_lo, w_hi[:], start=False, stop=True)

            def att_qkv(c, j):
                if j == 0:
                    need(pe, ayT_lo_made, c + 1)
                    if isinstance(c, int) and c == 0:
                        pe.wait_ge(weights_split, 9)
                elif isinstance(c, int) and c in (0, 1, NCH - 1):
                    need(pe, out_added, slot1(c) + 1)
                else:
                    need(pe, exp_made, slot1(c + 1) + 1)
                for i in range(2):
                    t = slice((2 * j + i) * P, (2 * j + i + 1) * P)
                    last = bias_and_split((ps_a, ps_f)[j][:, i * QKV:(i + 1) * QKV], ayT_hi[:, t], ayT_lo[:, t],
                                          wqkv_hi, wqkv_lo, slice(0, QKV))
                last.then_inc(qkv_ready, 1)

            def att_cum(c, i):
                if i % 2 == 0:
                    need(pe, kv_lo_made, 2 * c + i // 2 + 1)
                if i == 0:
                    need(pe, qkv_read, 2 * c + 2)
                else:
                    need(pe, cum_copied, TILES * c + i)
                parts = [(tri_r, kv_hi[:, i, :]), (tri_r, kv_lo[:, i, :])]
                if i % 2:
                    parts += [(ones_r, kv_hi[:, i - 1, :]), (ones_r, kv_lo[:, i - 1, :])]
                for k, (mask, part) in enumerate(parts):
                    last = pe.matmul(ps_a[:, 0:KVC], mask[:], part, start=(k == 0), stop=(k == len(parts) - 1))
                last.then_inc(cum_ready, 1)

            def end_oT(c):
                need(pe, o_made, c + 1)
                need(pe, cum_copied, TILES * (c + 1))
                for i in range(TILES):
                    last = pe.transpose(ps_a[:, i * P:(i + 1) * P], att_o[:, i, :], ident[:])
                last.then_inc(oT_ready, 1)

            def end_proj(c):
                need(pe, oT_lo_made, c + 1)
                for i in range(TILES):
                    t = slice(i * P, (i + 1) * P)
                    last = bias_and_split(ps_a[:, t], oT_hi[:, t], oT_lo[:, t], wo_hi, wo_lo, slice(QKV, QKV + D))
                last.then_inc(z_ready, 1)

            walk(pe, {"start_fold": start_fold, "in_yT": in_yT, "in_route": in_route, "in_wT": in_wT,
                      "ffn_up": ffn_up, "ffn_down": ffn_down, "ffn_w": ffn_w, "out_down": out_down, "out_T": out_T,
                      "att_yT": att_yT, "att_qkv": att_qkv, "att_cum": att_cum, "end_oT": end_oT,
                      "end_proj": end_proj})


_INS = ["L0_attn_x", "L0_attn_Wq", "L0_attn_bq", "L0_attn_Wk", "L0_attn_bk", "L0_attn_Wv", "L0_attn_bv",
        "L0_attn_Wc", "L0_attn_We", "L0_attn_Wo", "L0_attn_bo", "L0_attn_gamma", "L0_attn_beta",
        "L0_ffn_W_gate_router", "L0_ffn_expert_bias", "L0_ffn_Wg", "L0_ffn_Wu", "L0_ffn_Wd",
        "L0_ffn_Wg_s", "L0_ffn_Wu_s", "L0_ffn_Wd_s"]


def kernel(**inputs):
    import numpy as _np
    import concourse.bacc as _bacc
    from concourse import mybir as _mybir
    from concourse.bass_utils import run_bass_kernel_spmd as _run

    nc = _bacc.Bacc("TRN2", target_bir_lowering=False, num_devices=1)
    arrays, args = {}, []
    for name in _INS:
        a = _np.ascontiguousarray(inputs[name])
        arrays[f"in_{name}"] = a
        args.append(nc.dram_tensor(f"in_{name}", a.shape, _mybir.dt.from_np(a.dtype), kind="ExternalInput").ap())
    shape = inputs["L0_attn_x"].shape
    args.append(nc.dram_tensor("out_0", shape, _mybir.dt.float32, kind="ExternalOutput").ap())
    macaron_kernel(nc, *args)
    r = _run(nc, [arrays], core_ids=[0])
    return r.results[0]["out_0"]
```
